# Optimizing a Trainium2 kernel written in Bass

```python
import numpy as np
import jax
import jax.numpy as jnp

def _softmax(x, axis=-1):
    return jax.nn.softmax(x, axis=axis)

def _gelu(x):
    return jax.nn.gelu(x, approximate=True)

def _silu(x):
    return jax.nn.silu(x)

def _sigmoid(x):
    return jax.nn.sigmoid(x)

def _layernorm(x, axis=-1, eps=1e-05):
    m = jnp.mean(x, axis=axis, keepdims=True)
    v = jnp.var(x, axis=axis, keepdims=True)
    return (x - m) / jnp.sqrt(v + eps)

def _scatter_add(tgt, idx, src, axis=0):
    return tgt.at[idx].add(src)

def _segment_sum(src, seg, n):
    return jax.ops.segment_sum(src, seg, n)
kernel_name = 'mk_xattn_ffn_d1_seqx_r4_e16a37'

def setup_inputs(seed: int=0):
    np.random.seed(seed)
    _w = jnp.asarray

    def _rec_inputs():
        import jax
        import jax.numpy as jnp
        _rk = jax.random.key(seed)
        x = -0.0002928 + 1 * jax.random.normal(jax.random.fold_in(_rk, 1), (128, 128, 256), jnp.float32)
        _lenS = 128 - jax.random.randint(jax.random.fold_in(_rk, 7), (128,), 0, max(1, 128 // 4) + 1, jnp.int32)
        _lenS2 = 128 - jax.random.randint(jax.random.fold_in(_rk, 8), (128,), 0, max(1, 128 // 4) + 1, jnp.int32)
        _ctx_1024P = jax.random.normal(jax.random.fold_in(_rk, 11), (128, 16, 256), jnp.float32)
        _ctx_1024c = jax.random.dirichlet(jax.random.fold_in(_rk, 511), 0.3 * jnp.ones((16,), jnp.float32), (128, 128))
        _ctx_1024t = jnp.einsum('bsk,bkd->bsd', _ctx_1024c, _ctx_1024P)
        _ctx_1024t = _ctx_1024t * jax.lax.rsqrt(jnp.mean(jnp.square(_ctx_1024t)) + 1e-12) * 0.953939
        ctx_1024 = -1.39393e-06 + 0.999914 * (_ctx_1024t + 0.3 * jax.random.normal(jax.random.fold_in(_rk, 611), (128, 128, 256), jnp.float32))
        return (x, ctx_1024)
    x, ctx_1024 = _rec_inputs()

    def _L0_xattn_setup():
        import jax, jax.numpy as jnp
        import numpy as np
        B, T, D, H = (2, 512, 256, 16)
        DH = D // H
        key = jax.random.key(seed)
        ks = jax.random.split(key, 11)
        s = 1.0 / np.sqrt(D)
        return {'q': jax.random.normal(ks[0], (B, T, D), jnp.float32), 'k': jax.random.normal(ks[1], (B, T, D), jnp.float32), 'v': jax.random.normal(ks[2], (B, T, D), jnp.float32), 'wq_w': jax.random.normal(ks[3], (D, D), jnp.float32) * s, 'wq_b': jnp.zeros((D,), jnp.float32), 'wk_w': jax.random.normal(ks[4], (D, D), jnp.float32) * s, 'wk_b': jnp.zeros((D,), jnp.float32), 'wv_w': jax.random.normal(ks[5], (D, D), jnp.float32) * s, 'wv_b': jnp.zeros((D,), jnp.float32), 'wo_w': jax.random.normal(ks[6], (D, D), jnp.float32) * s, 'wo_b': jnp.zeros((D,), jnp.float32)}
    _L0_xattn_all = _L0_xattn_setup()
    _L0_xattn_in = {k: v for k, v in _L0_xattn_all.items() if k in ('wq_w', 'wq_b', 'wk_w', 'wk_b', 'wv_w', 'wv_b', 'wo_w', 'wo_b')}
    del _L0_xattn_all

    def _L0_ffn_setup():
        import jax, jax.numpy as jnp
        import numpy as np
        B, T, D, E, H = (8, 512, 256, 8, 64)
        LN_EPS = 1e-05
        key = jax.random.key(seed)
        ks = jax.random.split(key, 4)
        return {'x': jax.random.normal(ks[0], (B, T, D), dtype=jnp.float32), 'Wg': jax.random.normal(ks[1], (E, D), dtype=jnp.float32) * 0.02, 'ln_scale': jnp.ones((E, D), dtype=jnp.float32), 'ln_bias': jnp.zeros((E, D), dtype=jnp.float32), 'W1': jax.random.normal(ks[2], (E, D, H), dtype=jnp.float32) * 0.02, 'b1': jnp.zeros((E, H), dtype=jnp.float32), 'W2': jax.random.normal(ks[3], (E, H, D), dtype=jnp.float32) * 0.02, 'b2': jnp.zeros((E, D), dtype=jnp.float32)}
    _L0_ffn_all = _L0_ffn_setup()
    _L0_ffn_in = {k: v for k, v in _L0_ffn_all.items() if k in ('Wg', 'ln_scale', 'ln_bias', 'W1', 'b1', 'W2', 'b2')}
    del _L0_ffn_all
    return {'x': x, 'ctx_1024': ctx_1024, 'L0_xattn_wq_w': _L0_xattn_in['wq_w'], 'L0_xattn_wq_b': _L0_xattn_in['wq_b'], 'L0_xattn_wk_w': _L0_xattn_in['wk_w'], 'L0_xattn_wk_b': _L0_xattn_in['wk_b'], 'L0_xattn_wv_w': _L0_xattn_in['wv_w'], 'L0_xattn_wv_b': _L0_xattn_in['wv_b'], 'L0_xattn_wo_w': _L0_xattn_in['wo_w'], 'L0_xattn_wo_b': _L0_xattn_in['wo_b'], 'L0_ffn_Wg': _L0_ffn_in['Wg'], 'L0_ffn_ln_scale': _L0_ffn_in['ln_scale'], 'L0_ffn_ln_bias': _L0_ffn_in['ln_bias'], 'L0_ffn_W1': _L0_ffn_in['W1'], 'L0_ffn_b1': _L0_ffn_in['b1'], 'L0_ffn_W2': _L0_ffn_in['W2'], 'L0_ffn_b2': _L0_ffn_in['b2']}

def reference(x, ctx_1024, L0_xattn_wq_w, L0_xattn_wq_b, L0_xattn_wk_w, L0_xattn_wk_b, L0_xattn_wv_w, L0_xattn_wv_b, L0_xattn_wo_w, L0_xattn_wo_b, L0_ffn_Wg, L0_ffn_ln_scale, L0_ffn_ln_bias, L0_ffn_W1, L0_ffn_b1, L0_ffn_W2, L0_ffn_b2):
    import jax
    import jax.numpy as jnp

    def _L0_xattn_ref(q, k, v, wq_w, wq_b, wk_w, wk_b, wv_w, wv_b, wo_w, wo_b):
        import jax, jax.numpy as jnp
        import numpy as np
        B, T, D, H = (2, 512, 256, 16)
        DH = D // H
        b, t, d = q.shape
        wq = (q @ wq_w.T + wq_b).reshape(b, t, H, DH)
        wk = (k @ wk_w.T + wk_b).reshape(b, t, H, DH)
        wv = (v @ wv_w.T + wv_b).reshape(b, t, H, DH)
        scores = jnp.einsum('bthd,bshd->bhts', wq, wk) / jnp.sqrt(jnp.float32(DH))
        probs = jax.nn.softmax(scores, axis=-1)
        attn = jnp.einsum('bhts,bshd->bthd', probs, wv)
        attn = attn.reshape(b, t, d)
        return attn @ wo_w.T + wo_b

    def _L0_ffn_ref(x, Wg, ln_scale, ln_bias, W1, b1, W2, b2):
        import jax, jax.numpy as jnp
        import numpy as np
        B, T, D, E, H = (8, 512, 256, 8, 64)
        LN_EPS = 1e-05
        Bs, Ts, Ds = x.shape
        xt = x.reshape(Bs * Ts, Ds)
        logits = xt @ Wg.T
        top1 = jnp.argmax(logits, axis=-1)
        mu = jnp.mean(xt, axis=-1, keepdims=True)
        var = jnp.mean(jnp.square(xt - mu), axis=-1, keepdims=True)
        xhat = (xt - mu) * jax.lax.rsqrt(var + LN_EPS)
        n_experts = Wg.shape[0]

        def body(y, p):
            s_e, b_e, w1, bb1, w2, bb2, eid = p
            h = jax.nn.gelu((xhat * s_e + b_e) @ w1 + bb1, approximate=False)
            out = h @ w2 + bb2
            mask = (top1 == eid)[:, None].astype(out.dtype)
            return (y + mask * out, None)
        y0 = jnp.zeros_like(xt)
        y, _ = jax.lax.scan(body, y0, (ln_scale, ln_bias, W1, b1, W2, b2, jnp.arange(n_experts)))
        return y.reshape(Bs, Ts, Ds)
    x = x + _L0_xattn_ref(_layernorm(x, axis=-1), ctx_1024, ctx_1024, L0_xattn_wq_w, L0_xattn_wq_b, L0_xattn_wk_w, L0_xattn_wk_b, L0_xattn_wv_w, L0_xattn_wv_b, L0_xattn_wo_w, L0_xattn_wo_b)
    x = x + _L0_ffn_ref(_layernorm(x, axis=-1), L0_ffn_Wg, L0_ffn_ln_scale, L0_ffn_ln_bias, L0_ffn_W1, L0_ffn_b1, L0_ffn_W2, L0_ffn_b2)
    return x

_drawn_inputs = setup_inputs


def setup_inputs(seed=0):
    import zlib

    import numpy as np

    out = dict(_drawn_inputs(seed))
    spreads = {'L0_xattn_wq_b': (0.0, 0.327),
     'L0_xattn_wk_b': (0.0, 2.0),
     'L0_xattn_wv_b': (0.0, 0.1),
     'L0_xattn_wo_b': (0.0, 0.1),
     'L0_ffn_ln_scale': (1.0, 0.6),
     'L0_ffn_ln_bias': (0.0, 2.0),
     'L0_ffn_b1': (0.0, 0.8),
     'L0_ffn_b2': (0.0, 0.1)}
    factors = {}
    for name, (base, spread) in spreads.items():
        noise = np.random.default_rng([zlib.crc32(name.encode()), seed]).standard_normal(out[name].shape)
        drawn = base * np.exp(spread * noise) if base else spread * noise
        out[name] = jnp.asarray(drawn.astype(out[name].dtype))
    for name, factor in factors.items():
        out[name] = (out[name] * factor).astype(out[name].dtype)
    return out
```

```python
from contextlib import ExitStack

import concourse.bass as bass
from concourse import mybir

F32 = mybir.dt.float32
BF16 = mybir.dt.bfloat16
ALU = mybir.AluOpType
ACT = mybir.ActivationFunctionType
AX_X = mybir.AxisListType.X

P = 128
EPS = 1e-5
FAR = -float(2**30)


def at(pair, per_group, group, k):
    return pair * (2 * per_group) + (group * per_group + k)


def wait(engine, semaphore, value):
    if not isinstance(value, int) or value > 0:
        engine.wait_ge(semaphore, value)


def index(engine, value):
    return value if isinstance(value, int) else engine.snap(value)


def in_register(engine, value):
    return value if isinstance(value, int) else engine.to_reg(value)


def xattn_moe(nc, x, ctx_in, wq, bq, wk, bk, wv, bv, wo, bo, wg, ln_s, ln_b, w1, b1, w2, b2, out):
    BATCH, T, D = x.shape
    E, _, HID = w1.shape
    DH = 16
    H = D // DH
    C = D // P
    HC = H // C
    GB = 4
    GT = GB * T
    GROUPS = BATCH // GB
    PAIRS = GROUPS // 2
    UNITS = GB * C
    MC = E * HID // P
    EC = P // HID
    assert T == P and D == 256 and GROUPS % 2 == 0 and PAIRS > 2 and GROUPS * GB == BATCH

    Q_PARTS = (0, 0, 0, 1, 1, 2)
    K_PARTS = (0, 1, 2, 0, 1, 0)
    NPROD = len(Q_PARTS)
    KP = NPROD * DH
    PACK = 16 * NPROD * H
    ITEMS = 10

    x_v = x.rearrange("(g b) t d -> g t b d", b=GB)
    c_v = ctx_in.rearrange("(g b) t d -> g t b d", b=GB)
    out_v = out.rearrange("(g b) t d -> g t b d", b=GB)
    x2_dram = nc.dram_tensor("x2_scratch", [BATCH, T, D], F32, kind="Internal").ap()
    x2_v = x2_dram.rearrange("(g b) t d -> g t b d", b=GB)

    with ExitStack() as stack:
        def sb(name, shape, dt=F32):
            return stack.enter_context(nc.sbuf_tensor(name, shape, dt))

        def sem(name):
            return stack.enter_context(nc.semaphore(name))

        ident = sb("ident", [P, P])
        ident_bf = sb("ident_bf", [P, P], BF16)
        half_ones = sb("half_ones", [P, 2, 32])
        ones_row = sb("ones_row", [1, P])
        head_sel = sb("head_sel", [2 * HC, HC, P], BF16)
        far_sel = sb("far_sel", [E, MC * EC, HID], BF16)
        wqT, wkT, wvT, woT = (sb(n, [P, C, D]) for n in ("wqT", "wkT", "wvT", "woT"))
        w1s = sb("w1s", [P, C, E, HID])
        w2s = sb("w2s", [P, MC, D])
        rows = sb("rows", [3 * C + MC, P])
        cols = sb("cols", [P, 3 * C + MC])
        erows = sb("erows", [3 * E, D])
        ecols = sb("ecols", [P, C, 3 * E])
        c1 = sb("c1", [P, MC])
        bo_row = sb("bo_row", [1, D])
        bo_all = sb("bo_all", [P, D])
        b2f = sb("b2f", [E, D])
        b2r = sb("b2r", [E, D])
        b2p = sb("b2p", [E, 3, D], BF16)
        rank = sb("rank", [P, E])

        xin = sb("xin", [P, GB, D])
        cin = sb("cin", [P, GB, D])
        stats = sb("stats", [P, GB, 6])
        mv = sb("mv", [P, GB, 2])
        ve = sb("ve", [P, GB])
        rstd = sb("rstd", [P, GB])
        rstd2 = sb("rstd2", [P, GB])
        neg_half = sb("neg_half", [P, GB])
        eps = sb("eps", [P, GB])
        xn = sb("xn", [P, GB, D])
        xT = sb("xT", [P, C, GT])
        cT = sb("cT", [P, C, GT])
        z32 = [sb("q32", [P, C, GT]), sb("k32", [P, C, GT])]
        parts = [sb("q_parts", [P, 3, C, GT], BF16), sb("k_parts", [P, 3, C, GT], BF16)]
        packed = [[sb(f"{z}_packed{n}", [P, H, GT], BF16) for n in range(2)] for z in "qk"]
        vp = [sb(f"v{n}", [P, GB, H // 2, 64]) for n in range(2)]
        xb = [sb(f"xb{n}", [P, GB, D]) for n in range(2)]
        negmax = [sb(f"negmax{n}", [P, HC]) for n in range(2)]
        negmax_p = [sb(f"negmax_p{n}", [P, 2 * HC], BF16) for n in range(2)]
        negmaxT = [sb(f"negmaxT{n}", [2 * HC, P], BF16) for n in range(2)]
        pT = [sb(f"pT{n}", [P, HC * P]) for n in range(2)]
        recip = sb("recip", [P, C, P])
        aT = [sb(f"aT{n}", [P, C, P]) for n in range(2)]

        hT = [packed[0][n][:, :, :].rearrange("p h t -> p (h t)").bitcast(F32).rearrange(
            "p (m t) -> p m t", t=GT)[:, 0:MC, :] for n in range(2)]
        xhT = [packed[1][n][:, :, :].rearrange("p h t -> p (h t)").bitcast(F32).rearrange(
            "p (c t) -> p c t", t=GT)[:, 0:C, :] for n in range(2)]
        logit = sb("logit", [P, GB, E])
        top = sb("top", [P, GB])
        hit = sb("hit", [P, GB, E])
        first = sb("first", [P, GB, E])
        onehot = sb("onehot", [P, GB, E], BF16)
        onehotT = [sb(f"onehotT{n}", [E, GT], BF16) for n in range(2)]
        offhotT = [sb(f"offhotT{n}", [E, GT], BF16) for n in range(2)]

        def psum(name, shape, dt=F32):
            return stack.enter_context(nc.psum_tensor(name, shape, dt))

        s_ps = psum("s_ps", [P, 2 * 512])
        st_ps = psum("st_ps", [P, 2 * 512])
        pv_ps = psum("pv_ps", [P, C, 2, P])
        y_ps = psum("y_ps", [P, 512])
        pp_ps = [psum(f"pp_ps{n}", [P, 512]) for n in range(2)]

        s_small, s_w = sem("small_loaded"), sem("weights_loaded")
        s_const, s_wt, s_wtc = sem("constants"), sem("weight_transposed"), sem("weight_kept")
        s_set, s_pc = sem("dve_setup"), sem("pool_constant_step")
        ld_x, ld_c = sem("x_loaded"), sem("ctx_loaded")
        st_x2 = [sem(f"x2_stored{n}") for n in range(2)]
        pk = [[sem(f"{z}_packed_done{n}") for n in range(2)] for z in "qk"]
        s_bn, s_mv, s_ve, s_rstd, s_xn, s_xb = (sem(n) for n in (
            "bn_stats_done", "mean_var_done", "var_eps_done", "rstd_done", "xn_done", "xb_done"))
        s_pp, s_pe = sem("projection_in_psum"), sem("projection_kept")
        s_r, s_mid, s_lo = sem("remainder_done"), sem("mid_done"), sem("lo_done")
        s_s, s_red, s_hi, s_mp, s_mt, s_mte, s_st, s_exp, s_pv, s_rc, s_nrm = (sem(n) for n in (
            "scores_ready", "max_done", "max_hi_done", "max_parts_done", "max_transposed", "max_kept",
            "scoresT_ready", "exp_done", "pv_ready", "recip_done", "attn_normed"))
        s_y, s_x2 = sem("wo_ready"), sem("x2_done")

        CONSTS = 3 + E + 1 + 2 + 2 + 2
        SETUP_DVE = 12

        SLICES = [(0, 1, 2, 3), (4, 5), (6, 7), (8, 9), (), (), (), ()]
        MIDS = {2: 0, 3: 1}

        weight_banks = []
        for dst in (wqT, wkT, wvT, woT):
            weight_banks.append((dst[:].rearrange("p c d -> p (c d)"), C * D))
        weight_banks.append((cols[:], 3 * C + MC))
        weight_banks.append((ecols[:].rearrange("p c e -> p (c e)"), C * 3 * E))

        FIRST, LAST = 0, PAIRS - 1

        def pairs(engine, group_step):
            for n in range(2):
                group_step(FIRST, n, True, False)
            with engine.Fori(FIRST + 1, LAST) as pair:
                for n in range(2):
                    group_step(pair, n, False, False)
            for n in range(2):
                group_step(LAST, n, False, True)

        f_ld = [sem(f"ffn_x2_loaded{n}") for n in range(2)]
        f_st = [sem(f"ffn_out_stored{n}") for n in range(2)]
        (f_bn, f_mv, f_v1, f_r1, f_v2, f_v3, f_v4, f_r2, f_r12, f_xn) = (sem("ffn_" + n) for n in (
            "bn_stats", "mean_var", "var_eps", "rstd1", "var2a", "var2", "var2_eps", "rstd2", "rstd12", "xhat"))
        (f_tr, f_tre, f_g, f_gk, f_oh, f_ot, f_ote, f_h, f_he, f_y, f_out) = (sem("ffn_" + n) for n in (
            "xhatT_in_psum", "xhatT_kept", "logits_ready", "routing_step", "onehot_done", "onehotT_in_psum",
            "onehotT_kept", "hidden_in_psum", "hidden_kept", "out_in_psum", "out_done"))
        GK = 5
        tr_ps = pp_ps
        h_ps = [s_ps[:, 0:512], s_ps[:, 512:1024]]
        o_ps = [st_ps[:, 0:D], st_ps[:, 512:512 + D]]
        g_ps = y_ps[:, 0:GB * E]
        t_ps = pv_ps[:].rearrange("p a b t -> p (a b t)")[0:E, 0:GT // 2].bitcast(BF16)

        def ffn_sync(sp):
            def load(pair, n):
                src = x2_v[index(sp, pair * 2 + n)]
                wait(sp, f_st[n % 2], (pair + n // 2) * 16)
                sp.dma_start(xb[n % 2][:], src).then_inc(f_ld[n % 2], 16)

            def store(pair, n):
                dst = out_v[index(sp, pair * 2 + n)]
                sp.wait_ge(f_out, at(pair, GB, n, GB))
                sp.dma_start(dst, xb[n % 2][:]).then_inc(f_st[n % 2], 16)

            load(0, 0)
            load(0, 1)

            def group(pair, n, is_first, is_last):
                store(pair, n)
                if not is_last:
                    load(pair, n + 2)

            pairs(sp, group)
            for n in range(2):
                sp.wait_ge(f_st[n], 16 * PAIRS)

        def ffn_pool(pool):
            g = nc.gpsimd

            def norm(pair, n):
                one = at(pair, 1, n, 1)
                pool.wait_ge(f_mv, at(pair, GB, n, GB))
                g.tensor_tensor(ve[:], mv[:, :, 1], eps[:], ALU.add).then_inc(f_v1, 1)
                pool.wait_ge(f_v1, one)
                g.tensor_tensor(rstd[:], ve[:], neg_half[:], ALU.pow).then_inc(f_r1, 1)
                pool.wait_ge(f_r1, one)
                g.tensor_tensor(ve[:], mv[:, :, 1], rstd[:], ALU.mult).then_inc(f_v2, 1)
                pool.wait_ge(f_v2, one)
                g.tensor_tensor(rstd2[:], ve[:], rstd[:], ALU.mult).then_inc(f_v3, 1)
                pool.wait_ge(f_v3, one)
                g.tensor_tensor(ve[:], rstd2[:], eps[:], ALU.add).then_inc(f_v4, 1)
                pool.wait_ge(f_v4, one)
                g.tensor_tensor(rstd2[:], ve[:], neg_half[:], ALU.pow).then_inc(f_r2, 1)
                pool.wait_ge(f_r2, one)
                g.tensor_tensor(rstd[:], rstd[:], rstd2[:], ALU.mult).then_inc(f_r12, 1)

            norm(0, 0)

            def group(pair, n, is_first, is_last):
                if not (is_last and n == 1):
                    norm(pair, n + 1)

            pairs(pool, group)

        def ffn_act(act):
            a = nc.scalar

            def keep_xT(pair, n, c):
                act.wait_ge(f_tr, at(pair, C, n, c + 1))
                a.copy(xhT[n % 2][:, c, :], tr_ps[c][:]).then_inc(f_tre, 1)

            def keep_onehot(pair, n):
                act.wait_ge(f_ot, at(pair, 1, n, 1))
                a.copy(onehotT[n % 2][:], t_ps)
                a.activation(offhotT[n % 2][:], t_ps, ACT.Copy, bias=-1.0).then_inc(f_ote, 1)

            def gelu(pair, n, m):
                act.wait_ge(f_h, at(pair, MC, n, m + 1))
                a.activation(hT[n % 2][:, m, :], h_ps[m % 2], ACT.Gelu, bias=c1[:, m:m + 1]).then_inc(f_he, 1)

            for c in range(C):
                keep_xT(0, 0, c)
            keep_onehot(0, 0)

            def group(pair, n, is_first, is_last):
                for m in range(MC):
                    gelu(pair, n, m)
                if not (is_last and n == 1):
                    for c in range(C):
                        keep_xT(pair, n + 1, c)
                    keep_onehot(pair, n + 1)

            pairs(act, group)

        def ffn_dve(dve):
            v = nc.vector

            def stats_of(pair, n):
                dve.wait_ge(f_ld[n % 2], (pair + n // 2 + 1) * 16)
                for b in range(GB):
                    v.bn_stats(stats[:, b, :], xb[n % 2][:, b, :]).then_inc(f_bn, 1)
                for b in range(GB):
                    count = in_register(dve, at(pair, GB, n, b + 1))
                    dve.wait_ge(s_const, 1)
                    dve.wait_ge(f_bn, count)
                    v.bn_aggr(mv[:, b, :], stats[:, b, :]).then_inc(f_mv, 1)

            def normalise(pair, n):
                dve.wait_ge(f_r12, at(pair, 1, n, 1))
                wait(dve, f_tr, at(pair, C, n - 1, C))
                for b in range(GB):
                    v.tensor_scalar(xn[:, b, :], xb[n % 2][:, b, :], mv[:, b, 0:1], rstd[:, b:b + 1],
                                    ALU.subtract, ALU.mult).then_inc(f_xn, 1)

            def route(pair, n):
                dve.wait_ge(f_g, at(pair, 1, n, 1))
                lg = g_ps.rearrange("p (b e) -> p b e", e=E)
                topb = top[:].unsqueeze(2).broadcast_to([P, GB, E])
                v.tensor_reduce(top[:], lg, AX_X, ALU.max).then_inc(f_gk, 1)
                dve.wait_ge(f_gk, at(pair, GK, n, 1))
                v.tensor_tensor(hit[:], lg, topb, ALU.is_equal).then_inc(f_gk, 1)
                dve.wait_ge(f_gk, at(pair, GK, n, 2))
                v.tensor_tensor(first[:], hit[:], rank[:].unsqueeze(1).broadcast_to([P, GB, E]),
                                ALU.mult).then_inc(f_gk, 1)
                dve.wait_ge(f_gk, at(pair, GK, n, 3))
                v.tensor_reduce(top[:], first[:], AX_X, ALU.max).then_inc(f_gk, 1)
                dve.wait_ge(f_gk, at(pair, GK, n, 4))
                wait(dve, f_ot, at(pair, 1, n, 0))
                v.tensor_tensor(onehot[:], first[:], topb, ALU.is_equal).then_inc(f_gk, 1)

            def add(pair, n, b):
                dve.wait_ge(f_y, at(pair, GB, n, b + 1))
                xr = xb[n % 2][:, b, :]
                v.tensor_tensor(xr, xr, o_ps[b % 2], ALU.add).then_inc(f_out, 1)

            stats_of(0, 0)
            normalise(0, 0)
            route(0, 0)

            def group(pair, n, is_first, is_last):
                more = not (is_last and n == 1)
                if more:
                    stats_of(pair, n + 1)
                    normalise(pair, n + 1)
                add(pair, n, 0)
                add(pair, n, 1)
                if more:
                    route(pair, n + 1)
                add(pair, n, 2)
                add(pair, n, 3)

            pairs(dve, group)

        def ffn_pe(pe):
            t = nc.tensor

            def turn(pair, n, c):
                if c == 0:
                    pe.wait_ge(f_xn, at(pair, GB, n, GB))
                wait(pe, f_tre, at(pair, C, n - 1, c + 1))
                for b in range(GB):
                    mm = t.transpose(tr_ps[c][:, b * T:(b + 1) * T], xn[:, b, c * P:(c + 1) * P], ident[:])
                mm.then_inc(f_tr, 1)

            def gate(pair, n):
                pe.wait_ge(f_tre, at(pair, C, n, C))
                wait(pe, f_gk, at(pair, GK, n, 0))
                for b in range(GB):
                    for c in range(C):
                        mm = t.matmul(g_ps[:, b * E:(b + 1) * E], xhT[n % 2][:, c, b * T:(b + 1) * T],
                                      ecols[:, c, 0:E], start=(c == 0), stop=(c == C - 1))
                mm.then_inc(f_g, 1)

            def turn_onehot(pair, n):
                pe.wait_ge(f_gk, at(pair, GK, n, GK))
                wait(pe, f_ote, at(pair, 1, n, 0))
                for b in range(GB):
                    mm = t.transpose(t_ps[:, b * T:(b + 1) * T], onehot[:, b, :], ident_bf[:])
                mm.then_inc(f_ot, 1)

            def hidden(pair, n, m):
                if m == 0:
                    pe.wait_ge(f_ote, at(pair, 1, n, 1))
                wait(pe, f_he, at(pair, MC, n, m - 1))
                for c in range(C):
                    t.matmul(h_ps[m % 2], w1s[:, c, EC * m:EC * (m + 1), :], xhT[n % 2][:, c, :],
                             start=(c == 0), stop=False)
                t.matmul(h_ps[m % 2], far_sel[:, EC * m:EC * (m + 1), :], offhotT[n % 2][:],
                         start=False, stop=True).then_inc(f_h, 1)

            def output(pair, n, b):
                o = o_ps[b % 2]
                tok = slice(b * T, (b + 1) * T)
                pe.wait_ge(f_he, at(pair, MC, n, MC))
                wait(pe, f_out, at(pair, GB, n, b - 1))
                for m in range(MC):
                    t.matmul(o, hT[n % 2][:, m, tok], w2s[:, m, :], start=(m == 0), stop=False)
                for k in range(3):
                    mm = t.matmul(o, onehotT[n % 2][:, tok], b2p[:, k, :], start=False, stop=(k == 2))
                mm.then_inc(f_y, 1)

            pe.wait_ge(s_x2, GROUPS * GB)
            for c in range(C):
                turn(0, 0, c)
            gate(0, 0)
            turn_onehot(0, 0)

            def group(pair, n, is_first, is_last):
                more = not (is_last and n == 1)
                for m in range(MC):
                    hidden(pair, n, m)
                for b in range(GB):
                    output(pair, n, b)
                    if b == 1 and more:
                        for c in range(C):
                            turn(pair, n + 1, c)
                        gate(pair, n + 1)
                if more:
                    turn_onehot(pair, n + 1)

            pairs(pe, group)

        block = stack.enter_context(nc.Block())

        @block.sync
        def _(sp):
            def load_x(pair, g):
                src = x_v[index(sp, pair * 2 + g)]
                wait(sp, s_xb, at(pair, 1, g - 1, 1))
                sp.dma_start(xin[:], src).then_inc(ld_x, 16)

            def load_c(pair, g):
                src = c_v[index(sp, pair * 2 + g)]
                wait(sp, s_pp, at(pair, ITEMS, g - 1, 4))
                sp.dma_start(cin[:], src).then_inc(ld_c, 16)

            def store_x2(pair, g):
                dst = x2_v[index(sp, pair * 2 + g)]
                wait(sp, s_x2, at(pair, GB, g, GB))
                sp.dma_start(dst, xb[g % 2][:]).then_inc(st_x2[g % 2], 16)

            def pack(pair, g, z):
                wait(sp, s_lo, at(pair, 2, g, z + 1))
                for h in range(H):
                    rows_of = slice(h % HC * DH, h % HC * DH + DH)
                    for n, part in enumerate((Q_PARTS, K_PARTS)[z]):
                        sp.dma_start(packed[z][g % 2][n * DH:(n + 1) * DH, h, :],
                                     parts[z][rows_of, part, h // HC, :]).then_inc(pk[z][g % 2], 16)

            for n, v in enumerate((bq, bk, bv)):
                sp.dma_start(rows[n * C:(n + 1) * C, :], v.rearrange("(c p) -> c p", p=P)).then_inc(s_small, 16)
            sp.dma_start(rows[3 * C:3 * C + MC, :], b1.rearrange("(m e) h -> m (e h)", e=EC)).then_inc(s_small, 16)
            for n, v in enumerate((wg, ln_s, ln_b)):
                sp.dma_start(erows[n * E:(n + 1) * E, :], v).then_inc(s_small, 16)
            sp.dma_start(bo_row[:], bo.rearrange("(a d) -> a d", a=1)).then_inc(s_small, 16)
            sp.dma_start(b2f[:], b2).then_inc(s_small, 16)
            for v, t in ((wq, xn[:, 0:C, :]), (wk, xn[:, C:2 * C, :]),
                         (wv, z32[0][:, 0, :].rearrange("p (c d) -> p c d", c=C)),
                         (wo, z32[0][:, 1, :].rearrange("p (c d) -> p c d", c=C))):
                sp.dma_start(t, v.rearrange("(c p) d -> p c d", p=P)).then_inc(s_w, 16)
            for c in range(C):
                sp.dma_start(w1s[:, c, :, :], w1[:, c * P:(c + 1) * P, :].rearrange("e p h -> p e h")).then_inc(s_w, 16)
            sp.dma_start(w2s[:], w2.rearrange("(m e) h d -> (e h) m d", e=EC) if False else
                         w2.rearrange("e h d -> (e h) d").rearrange("(m p) d -> p m d", p=P)).then_inc(s_w, 16)

            load_x(0, 0)
            load_c(0, 0)
            load_x(0, 1)
            pack(0, 0, 0)
            pack(0, 0, 1)
            load_c(0, 1)

            def group(pair, g, is_first, is_last):
                if not (is_first and g == 0):
                    store_x2(pair, g - 1)
                if not is_last:
                    load_x(pair, g + 2)
                if not (is_last and g == 1):
                    if not is_last:
                        load_c(pair, g + 2)
                    pack(pair, g + 1, 0)
                    pack(pair, g + 1, 1)

            pairs(sp, group)
            store_x2(LAST, 1)
            for n in range(2):
                sp.wait_ge(st_x2[n], 16 * PAIRS)
            ffn_sync(sp)

        @block.gpsimd
        def _(pool):
            g = nc.gpsimd
            g.memset(ident[:], 0.0).then_inc(s_pc, 1)
            g.memset(head_sel[:], 0.0).then_inc(s_pc, 1)
            g.memset(far_sel[:], 0.0).then_inc(s_pc, 1)
            g.memset(neg_half[:], -0.5).then_inc(s_const, 1)
            g.memset(eps[:], EPS).then_inc(s_const, 1)
            g.memset(ones_row[:], 1.0).then_inc(s_const, 1)
            g.memset(half_ones[:], 0.0).then_inc(s_pc, 1)
            for e in range(E):
                g.memset(rank[:, e:e + 1], float(E - e)).then_inc(s_const, 1)
            pool.wait_ge(s_pc, 4)
            g.affine_select(out=ident[:], in_=ident[:], compare_op=ALU.not_equal, fill=1.0, base=0,
                            pattern=[[-1, P]], channel_multiplier=1).then_inc(s_pc, 1)
            g.affine_select(out=head_sel[:], in_=head_sel[:], compare_op=ALU.not_equal, fill=1.0, base=0,
                            pattern=[[-1, HC], [0, P]], channel_multiplier=1).then_inc(s_pc, 1)
            g.affine_select(out=far_sel[:], in_=far_sel[:], compare_op=ALU.not_equal, fill=-FAR, base=0,
                            pattern=[[-1, MC * EC], [0, HID]], channel_multiplier=1).then_inc(s_const, 1)
            for e in range(2):
                g.memset(half_ones[:, e, 16 * e:16 * e + 16], 1.0).then_inc(s_const, 1)
            for n in range(2):
                g.memset(vp[n][:], 0.0).then_inc(s_const, 1)
            pool.wait_ge(s_pc, 6)
            g.affine_select(out=head_sel[:], in_=head_sel[:], compare_op=ALU.not_equal, fill=1.0, base=-HC,
                            pattern=[[-1, HC], [0, P]], channel_multiplier=1).then_inc(s_const, 1)
            g.tensor_copy(ident_bf[:], ident[:]).then_inc(s_const, 1)

            def norm(pair, n):
                pool.wait_ge(s_mv, at(pair, GB, n, GB))
                g.tensor_tensor(ve[:], mv[:, :, 1], eps[:], ALU.add).then_inc(s_ve, 1)
                pool.wait_ge(s_ve, at(pair, 1, n, 1))
                g.tensor_tensor(rstd[:], ve[:], neg_half[:], ALU.pow).then_inc(s_rstd, 1)

            def residual(pair, n):
                pool.wait_ge(s_xn, at(pair, GB, n, GB))
                wait(pool, st_x2[n % 2], (pair + n // 2) * 16)
                for b in range(GB):
                    last = g.tensor_tensor(xb[n % 2][:, b, :], xin[:, b, :], bo_all[:], ALU.add)
                last.then_inc(s_xb, 1)

            norm(0, 0)
            pool.wait_ge(s_set, SETUP_DVE)
            residual(0, 0)
            norm(0, 1)
            residual(0, 1)

            def group(pair, n, is_first, is_last):
                if not is_last:
                    norm(pair, n + 2)
                    residual(pair, n + 2)

            pairs(pool, group)
            ffn_pool(pool)

        @block.scalar
        def _(act):
            a = nc.scalar

            def keep_max(pair, n, u):
                act.wait_ge(s_mt, at(pair, UNITS, n, u + 1))
                a.copy(negmaxT[u % 2][:], y_ps[0:2 * HC, 256:320].bitcast(BF16)).then_inc(s_mte, 1)

            def item(pair, n, k):
                act.wait_ge(s_pp, at(pair, ITEMS, n, k + 1))
                ps = pp_ps[k % 2]
                if k < 4:
                    last = a.copy((xT, cT)[k // 2][:, k % 2, :], ps[:])
                elif k < 8:
                    z, m = (k - 4) // 2, k % 2
                    if m == 0:
                        wait(act, s_lo, at(pair, 2, n - 1, z + 1))
                        wait(act, pk[z][(n - 1) % 2], (pair + (n - 1) // 2 + 1) * PACK)
                    bias = cols[:, z * C + m:z * C + m + 1]
                    a.activation(z32[z][:, m, :], ps[:], ACT.Identity, bias=bias)
                    last = a.activation(parts[z][:, 0, m, :], ps[:], ACT.Identity, bias=bias)
                else:
                    b = 2 * (k - 8)
                    src = ps[:].rearrange("p (b q e d) -> p b q e d", b=2, e=2, d=DH)
                    for e in range(2):
                        last = a.copy(vp[n % 2][:, b:b + 2, :, 48 * e:48 * e + DH], src[:, :, :, e, :])
                last.then_inc(s_pe, 1)

            def mid(pair, n, z):
                act.wait_ge(s_r, at(pair, 2, n, z + 1))
                a.copy(parts[z][:, 1, :, :], z32[z][:]).then_inc(s_mid, 1)

            def exp(pair, n, u):
                act.wait_ge(s_st, at(pair, UNITS, n, u + 1))
                wait(act, s_pv, at(pair, UNITS, n, u - 1))
                a.activation(pT[u % 2][:], st_ps[:], ACT.Exp, scale=DH ** -0.5).then_inc(s_exp, 1)

            for k, (dst, width) in enumerate(weight_banks):
                act.wait_ge(s_wt, k + 1)
                a.copy(dst, pp_ps[k % 2][0:P, 0:width]).then_inc(s_wtc, 1)
            act.wait_ge(s_set, SETUP_DVE)

            for k in range(ITEMS):
                item(0, 0, k)
                if k == 8:
                    mid(0, 0, 0)
            mid(0, 0, 1)

            def group(pair, n, is_first, is_last):
                more = not (is_last and n == 1)
                for u in range(UNITS):
                    keep_max(pair, n, u)
                    if more:
                        for k in SLICES[u]:
                            item(pair, n + 1, k)
                    exp(pair, n, u)
                    if more and u in MIDS:
                        mid(pair, n + 1, MIDS[u])

            pairs(act, group)
            ffn_act(act)

        @block.vector
        def _(dve):
            v = nc.vector
            step = [0]

            def setup(ins):
                step[0] += 1
                ins.then_inc(s_set, 1)
                dve.wait_ge(s_set, step[0])

            def stats_of(pair, n):
                dve.wait_ge(ld_x, at(pair, 16, n, 16))
                for b in range(GB):
                    v.bn_stats(stats[:, b, :], xin[:, b, :]).then_inc(s_bn, 1)
                for b in range(GB):
                    count = in_register(dve, at(pair, GB, n, b + 1))
                    dve.wait_ge(s_const, 1)
                    dve.wait_ge(s_bn, count)
                    v.bn_aggr(mv[:, b, :], stats[:, b, :]).then_inc(s_mv, 1)

            def normalise(pair, n):
                dve.wait_ge(s_rstd, at(pair, 1, n, 1))
                wait(dve, s_pp, at(pair, ITEMS, n - 1, 2))
                for b in range(GB):
                    v.tensor_scalar(xn[:, b, :], xin[:, b, :], mv[:, b, 0:1], rstd[:, b:b + 1],
                                    ALU.subtract, ALU.mult).then_inc(s_xn, 1)

            def remainder(pair, n, z):
                dve.wait_ge(s_pe, at(pair, ITEMS, n, 6 + 2 * z))
                v.tensor_tensor(z32[z][:], z32[z][:], parts[z][:, 0, :, :], ALU.subtract).then_inc(s_r, 1)

            def lo(pair, n, z):
                dve.wait_ge(s_mid, at(pair, 2, n, z + 1))
                v.tensor_tensor(parts[z][:, 2, :, :], z32[z][:], parts[z][:, 1, :, :],
                                ALU.subtract).then_inc(s_lo, 1)

            def maxima(pair, n, u):
                dve.wait_ge(s_s, at(pair, UNITS, n, u + 1))
                v.tensor_reduce(negmax[u % 2][:], s_ps[:].rearrange("p (h s) -> p h s", s=P), AX_X, ALU.max,
                                negate=True).then_inc(s_red, 1)
                dve.wait_ge(s_red, at(pair, UNITS, n, u + 1))
                wait(dve, s_mt, at(pair, UNITS, n, u - 1))
                v.tensor_copy(negmax_p[u % 2][:, 0:HC], negmax[u % 2][:]).then_inc(s_hi, 1)
                dve.wait_ge(s_hi, at(pair, UNITS, n, u + 1))
                v.tensor_tensor(negmax_p[u % 2][:, HC:2 * HC], negmax[u % 2][:], negmax_p[u % 2][:, 0:HC],
                                ALU.subtract).then_inc(s_mp, 1)

            def norm(pair, n, b):
                dve.wait_ge(s_pv, at(pair, UNITS, n, C * (b + 1)))
                v.reciprocal(recip[:], pv_ps[:, :, 1, :]).then_inc(s_rc, 1)
                dve.wait_ge(s_rc, at(pair, GB, n, b + 1))
                wait(dve, s_y, at(pair, GB, n, b - 1))
                v.tensor_tensor(aT[b % 2][:], pv_ps[:, :, 0, :], recip[:], ALU.mult).then_inc(s_nrm, 1)

            def residual(pair, n, b):
                dve.wait_ge(s_y, at(pair, GB, n, b + 1))
                if b == 0:
                    dve.wait_ge(s_xb, at(pair, 1, n, 1))
                xr = xb[n % 2][:, b, :]
                v.tensor_tensor(xr, xr, y_ps[:, 0:D], ALU.add).then_inc(s_x2, 1)

            stats_of(0, 0)
            dve.wait_ge(s_wt, len(weight_banks) + 1)
            dve.wait_ge(s_wtc, len(weight_banks))
            for m in range(MC):
                for e in range(EC):
                    r = slice(e * HID, (e + 1) * HID)
                    v.tensor_tensor(c1[r, m:m + 1], pp_ps[0][r, EC * m + e:EC * m + e + 1],
                                    cols[r, 3 * C + m:3 * C + m + 1], ALU.add)
            for c in range(C):
                ls = ecols[:, c, E:2 * E].unsqueeze(2).broadcast_to([P, E, HID])
                setup(v.tensor_tensor(w1s[:, c, :, :], w1s[:, c, :, :], ls, ALU.mult))
            setup(v.tensor_copy(b2p[:, 0, :], b2f[:]))
            setup(v.tensor_tensor(b2r[:], b2f[:], b2p[:, 0, :], ALU.subtract))
            setup(v.tensor_copy(b2p[:, 1, :], b2r[:]))
            setup(v.tensor_tensor(b2p[:, 2, :], b2r[:], b2p[:, 1, :], ALU.subtract))
            dve.wait_ge(s_wt, len(weight_banks) + 2)
            setup(v.tensor_copy(bo_all[:], pp_ps[1][:, 0:D]))
            while step[0] < SETUP_DVE:
                setup(v.tensor_copy(recip[:, 0, 0:1], bo_all[:, 0:1]))

            normalise(0, 0)
            remainder(0, 0, 0)
            remainder(0, 0, 1)
            lo(0, 0, 0)
            lo(0, 0, 1)
            stats_of(0, 1)
            normalise(0, 1)
            maxima(0, 0, 0)

            def group(pair, n, is_first, is_last):
                more = not (is_last and n == 1)
                for u in range(UNITS):
                    if u + 1 < UNITS:
                        maxima(pair, n, u + 1)
                    elif more:
                        maxima(pair, n + 1, 0)
                    if u % 2 == 0:
                        if u > 0:
                            norm(pair, n, u // 2 - 1)
                        elif not (is_first and n == 0):
                            norm(pair, n - 1, GB - 1)
                    else:
                        if u > 1:
                            residual(pair, n, u // 2 - 1)
                        elif not (is_first and n == 0):
                            residual(pair, n - 1, GB - 1)
                    if more:
                        if u == 1:
                            remainder(pair, n + 1, 0)
                        if u == 2:
                            lo(pair, n + 1, 0)
                            remainder(pair, n + 1, 1)
                        if u == 3:
                            lo(pair, n + 1, 1)
                    if not is_last:
                        if u == 5:
                            stats_of(pair, n + 2)
                        if u == 6:
                            normalise(pair, n + 2)

            pairs(dve, group)
            norm(LAST, 1, GB - 1)
            residual(LAST, 1, GB - 1)
            ffn_dve(dve)

        @block.tensor
        def _(pe):
            t = nc.tensor

            def scores(pair, n, u):
                b, m = u // C, u % C
                tok = slice(b * T, (b + 1) * T)
                if u == 0:
                    for z in range(2):
                        pe.wait_ge(pk[z][n % 2], (pair + n // 2 + 1) * PACK)
                wait(pe, s_red, at(pair, UNITS, n, u))
                for j in range(HC):
                    h = m * HC + j
                    mm = t.matmul(s_ps[:, j * P:(j + 1) * P], packed[0][n % 2][0:KP, h, tok],
                                  packed[1][n % 2][0:KP, h, tok], start=True, stop=True)
                mm.then_inc(s_s, 1)

            def turn_max(pair, n, u):
                pe.wait_ge(s_mp, at(pair, UNITS, n, u + 1))
                if u % 2 == 0:
                    wait(pe, s_x2, at(pair, GB, n, u // 2 - 1))
                t.transpose(y_ps[0:2 * HC, 256:320].bitcast(BF16), negmax_p[u % 2][:], ident_bf[:]).then_inc(s_mt, 1)

            def scoresT(pair, n, u):
                b, m = u // C, u % C
                tok = slice(b * T, (b + 1) * T)
                pe.wait_ge(s_mte, at(pair, UNITS, n, u + 1))
                wait(pe, s_exp, at(pair, UNITS, n, u))
                for j in range(HC):
                    h = m * HC + j
                    o = st_ps[:, j * P:(j + 1) * P]
                    t.matmul(o, packed[1][n % 2][0:KP, h, tok], packed[0][n % 2][0:KP, h, tok],
                             start=True, stop=False)
                    mm = t.matmul(o, head_sel[:, j, :], negmaxT[u % 2][:], start=False, stop=True)
                mm.then_inc(s_st, 1)

            def values(pair, n, u):
                b, m = u // C, u % C
                pe.wait_ge(s_exp, at(pair, UNITS, n, u + 1))
                if m == 0:
                    wait(pe, s_nrm, at(pair, GB, n, b))
                if u == 0:
                    pe.wait_ge(s_pe, at(pair, ITEMS, n, ITEMS))
                for what in range(2):
                    for e in range(2):
                        for j in range(4):
                            col = (2 * j + e) * P
                            w = vp[n % 2][:, b, 4 * m + j, 32 * e:32 * e + 32] if what == 0 else half_ones[:, e, :]
                            mm = t.matmul(pv_ps[32 * j:32 * j + 32, m, what, :], w,
                                          pT[u % 2][:, col:col + P], start=(e == 0), stop=(e == 1))
                mm.then_inc(s_pv, 1)

            def project_out(pair, n, b):
                pe.wait_ge(s_nrm, at(pair, GB, n, b + 1))
                for c in range(C):
                    mm = t.matmul(y_ps[:, 0:D], aT[b % 2][:, c, :], woT[:, c, :], start=(c == 0), stop=(c == C - 1))
                mm.then_inc(s_y, 1)

            def item(pair, n, k):
                ps = pp_ps[k % 2]
                if k == 0:
                    pe.wait_ge(s_xn, at(pair, GB, n, GB))
                if k == 2:
                    pe.wait_ge(ld_c, at(pair, 16, n, 16))
                wait(pe, s_pe, at(pair, ITEMS, n, k - 1))
                if k < 4:
                    for b in range(GB):
                        mm = t.transpose(ps[:, b * T:(b + 1) * T],
                                         (xn, cin)[k // 2][:, b, k % 2 * P:(k % 2 + 1) * P], ident[:])
                elif k < 8:
                    w, src = ((wqT, xT), (wkT, cT))[(k - 4) // 2]
                    for c in range(C):
                        mm = t.matmul(ps[:], w[:, c, k % 2 * P:(k % 2 + 1) * P], src[:, c, :],
                                      start=(c == 0), stop=(c == C - 1))
                else:
                    for b in range(2):
                        tok = (2 * (k - 8) + b) * T
                        for c in range(C):
                            mm = t.matmul(ps[:, b * D:(b + 1) * D], cT[:, c, tok:tok + T], wvT[:, c, :],
                                          start=(c == 0), stop=(c == C - 1))
                mm.then_inc(s_pp, 1)

            pe.wait_ge(s_const, CONSTS)
            pe.wait_ge(s_small, 16 * 9)
            pe.wait_ge(s_w, 16 * 7)
            sources = [xn[:, 0:C, :], xn[:, C:2 * C, :], z32[0][:, 0, :].rearrange("p (c d) -> p c d", c=C),
                       z32[0][:, 1, :].rearrange("p (c d) -> p c d", c=C)]
            for k, w in enumerate(sources):
                if k >= 2:
                    pe.wait_ge(s_wtc, k - 1)
                for ci in range(C):
                    for co in range(C):
                        mm = t.transpose(pp_ps[k % 2][:, ci * D + co * P:ci * D + (co + 1) * P],
                                         w[:, co, ci * P:(ci + 1) * P], ident[:])
                mm.then_inc(s_wt, 1)
            pe.wait_ge(s_wtc, 3)
            NR = 3 * C + MC
            t.transpose(pp_ps[0][:, 0:NR], rows[:], ident[0:NR, 0:NR]).then_inc(s_wt, 1)
            pe.wait_ge(s_wtc, 4)
            for c in range(C):
                mm = t.transpose(pp_ps[1][:, c * 3 * E:(c + 1) * 3 * E], erows[:, c * P:(c + 1) * P],
                                 ident[0:3 * E, 0:3 * E])
            mm.then_inc(s_wt, 1)
            pe.wait_ge(s_wtc, 6)
            for m in range(MC):
                for c in range(C):
                    mm = t.matmul(pp_ps[0][:, EC * m:EC * (m + 1)], w1s[:, c, EC * m:EC * (m + 1), :],
                                  ecols[:, c, 2 * E + EC * m:2 * E + EC * (m + 1)], start=(c == 0), stop=(c == C - 1))
            mm.then_inc(s_wt, 1)
            for c in range(C):
                t.matmul(pp_ps[1][:, 0:D], cols[:, 2 * C + c:2 * C + c + 1].broadcast_to([P, P]), woT[:, c, :],
                         start=(c == 0), stop=False)
            t.matmul(pp_ps[1][:, 0:D], ones_row[:], bo_row[:], start=False, stop=True).then_inc(s_wt, 1)
            pe.wait_ge(s_set, SETUP_DVE)

            for k in range(ITEMS):
                item(0, 0, k)
            scores(0, 0, 0)

            def group(pair, n, is_first, is_last):
                more = not (is_last and n == 1)
                for u in range(UNITS):
                    if u + 1 < UNITS:
                        scores(pair, n, u + 1)
                    elif more:
                        scores(pair, n + 1, 0)
                    turn_max(pair, n, u)
                    if more:
                        for k in SLICES[u]:
                            item(pair, n + 1, k)
                    scoresT(pair, n, u)
                    if u > 0:
                        values(pair, n, u - 1)
                    elif not (is_first and n == 0):
                        values(pair, n - 1, UNITS - 1)
                    if u % 2 == 1:
                        if u > 1:
                            project_out(pair, n, u // 2 - 1)
                        elif not (is_first and n == 0):
                            project_out(pair, n - 1, GB - 1)

            pairs(pe, group)
            values(LAST, 1, UNITS - 1)
            project_out(LAST, 1, GB - 1)
            ffn_pe(pe)


_INS = ['x', 'ctx_1024'] + ['L0_xattn_' + n for n in ('wq_w', 'wq_b', 'wk_w', 'wk_b', 'wv_w', 'wv_b', 'wo_w', 'wo_b')] + \
    ['L0_ffn_' + n for n in ('Wg', 'ln_scale', 'ln_bias', 'W1', 'b1', 'W2', 'b2')]


def kernel(**inputs):
    import numpy as _np
    import concourse.bacc as _bacc
    from concourse import mybir as _mybir
    from concourse.bass_utils import run_bass_kernel_spmd as _run

    nc = _bacc.Bacc("TRN2", target_bir_lowering=False, num_devices=1)
    arrays, args = {}, []
    for name in _INS:
        a = _np.ascontiguousarray(inputs[name])
        arrays[f"in_{name}_dram"] = a
        args.append(nc.dram_tensor(f"in_{name}_dram", a.shape, _mybir.dt.from_np(a.dtype), kind="ExternalInput").ap())
    shape = inputs["x"].shape
    args.append(nc.dram_tensor("out_0_dram", shape, _mybir.dt.float32, kind="ExternalOutput").ap())
    xattn_moe(nc, *args)
    r = _run(nc, [arrays], core_ids=[0])
    return r.results[0]["out_0_dram"]
```

```python
from contextlib import ExitStack

import concourse.bass as bass
from concourse import mybir

F32 = mybir.dt.float32
F32R = mybir.dt.float32r
BF16 = mybir.dt.bfloat16
ALU = mybir.AluOpType
ACT = mybir.ActivationFunctionType
AX_X = mybir.AxisListType.X

P = 128
EPS = 1e-5
FAR = -float(2**30)


def at(pair, per_group, group, k):
    return pair * (2 * per_group) + (group * per_group + k)


def wait(engine, semaphore, value):
    if not isinstance(value, int) or value > 0:
        engine.wait_ge(semaphore, value)


def index(engine, value):
    return value if isinstance(value, int) else engine.snap(value)


def in_register(engine, value):
    return value if isinstance(value, int) else engine.to_reg(value)


def xattn_moe(nc, x, ctx_in, wq, bq, wk, bk, wv, bv, wo, bo, wg, ln_s, ln_b, w1, b1, w2, b2, out):
    BATCH, T, D = x.shape
    E, _, HID = w1.shape
    DH = 16
    H = D // DH
    C = D // P
    HC = H // C
    GB = 4
    GT = GB * T
    GROUPS = BATCH // GB
    PAIRS = GROUPS // 2
    UNITS = GB * C
    MC = E * HID // P
    EC = P // HID
    assert T == P and D == 256 and GROUPS % 2 == 0 and PAIRS > 2 and GROUPS * GB == BATCH

    Q_PARTS = (0, 0, 0, 1, 1, 2)
    K_PARTS = (0, 1, 2, 0, 1, 0)
    NPROD = len(Q_PARTS)
    KP = NPROD * DH
    PACK = 16 * NPROD
    EP = 32
    HP = 2 * DH
    ITEMS = 10

    x_v = x.rearrange("(g b) t d -> g t b d", b=GB)
    c_v = ctx_in.rearrange("(g b) t d -> g t b d", b=GB)
    out_v = out.rearrange("(g b) t d -> g t b d", b=GB)
    parts_dram = [[nc.dram_tensor(f"{z}_parts_scratch{n}", [3, D, GT], BF16, kind="Internal").ap()
                   for n in range(2)] for z in "qk"]
    x2_dram = nc.dram_tensor("x2_scratch", [BATCH, T, D], F32, kind="Internal").ap()
    x2_v = x2_dram.rearrange("(g b) t d -> g t b d", b=GB)

    with ExitStack() as stack:
        def sb(name, shape, dt=F32):
            return stack.enter_context(nc.sbuf_tensor(name, shape, dt))

        def sem(name):
            return stack.enter_context(nc.semaphore(name))

        ident = sb("ident", [P, P])
        ident_bf = sb("ident_bf", [P, P], BF16)
        ones_row = sb("ones_row", [1, P])
        head_sel = sb("head_sel", [P, HC, P], BF16)
        far_sel = sb("far_sel", [E, MC * EC, HID], BF16)
        wqT, wkT, wvT, woT = (sb(n, [P, C, D]) for n in ("wqT", "wkT", "wvT", "woT"))
        w1_hi, w1_lo = (sb(n, [P, C, E, HID]) for n in ("w1_hi", "w1_lo"))
        w2_hi, w2_lo = (sb(n, [P, MC, D]) for n in ("w2_hi", "w2_lo"))
        rows = sb("rows", [3 * C + MC, P])
        cols = sb("cols", [P, 3 * C + MC])
        erows = sb("erows", [3 * E, D])
        ecols = sb("ecols", [P, C, 3 * E])
        wg_pad = sb("wg_pad", [P, C, EP])
        c1 = sb("c1", [P, MC])
        bo_row = sb("bo_row", [1, D])
        bo_all = sb("bo_all", [P, D])
        b2f = sb("b2f", [3 * EP, D])
        b2r = sb("b2r", [3 * EP, D])
        b2p = sb("b2p", [3 * EP, D], BF16)
        rank = sb("rank", [P, E])

        xin = [sb(f"xin{n}", [P, GB, D]) for n in range(2)]
        cin = sb("cin", [P, GB, D])
        stats = sb("stats", [P, GB, 6])
        mv = sb("mv", [P, GB, 2])
        ve = sb("ve", [P, GB])
        rstd = sb("rstd", [P, GB])
        rstd2 = sb("rstd2", [P, GB])
        neg_half = sb("neg_half", [P, GB])
        eps = sb("eps", [P, GB])
        xn = sb("xn", [P, GB, D])
        xT = sb("xT", [P, C, GT])
        cT = sb("cT", [P, C, GT])
        z32 = [sb("q32", [P, C, GT]), sb("k32", [P, C, GT])]
        parts = [sb("q_parts", [P, 3, C, GT], BF16), sb("k_parts", [P, 3, C, GT], BF16)]
        packed = [[sb(f"{z}_packed{n}", [P, H, GT], BF16) for n in range(2)] for z in "qk"]
        v1 = [sb(f"v{n}", [P, GB, H, HP]) for n in range(2)]
        xb = [sb(f"xb{n}", [P, GB, D]) for n in range(2)]
        negmax = [sb(f"negmax{n}", [P, HC]) for n in range(2)]
        negmax_p = [sb(f"negmax_p{n}", [P, 2 * HC], BF16) for n in range(2)]
        negmaxT = [sb(f"negmaxT{n}", [P, P], BF16) for n in range(2)]
        pT = [sb(f"pT{n}", [P, HC * P]) for n in range(2)]
        w1s = pT[1][:].rearrange("p (c e h) -> p c e h", c=C, e=E)
        w2s = pT[0][:].rearrange("p (m d) -> p m d", m=MC)
        recip = sb("recip", [P, H])
        uvT = sb("uvT", [P, 512])
        attn = sb("attn", [P, H, DH])
        aT = [sb(f"aT{n}", [P, C, P]) for n in range(2)]

        def rows_of(packed_n):
            return packed_n[:, :, :].rearrange("p h t -> p (h t)").bitcast(F32).rearrange("p (m t) -> p m t", t=GT)

        hT_hi, hT_lo = ([rows_of(packed[0][n])[:, k * MC:(k + 1) * MC, :] for n in range(2)] for k in range(2))
        xhT_hi, xhT_lo = ([rows_of(packed[1][n])[:, k * C:(k + 1) * C, :] for n in range(2)] for k in range(2))
        xhT = z32
        hidden32 = [pT[m // 2][:, m % 2 * GT:(m % 2 + 1) * GT] for m in range(MC)]
        logitT = sb("logitT", [P, P])
        top = sb("top", [P, GB])
        hit = sb("hit", [P, GB, E])
        first = sb("first", [P, GB, E])
        onehot = sb("onehot", [P, GB, 3, EP], BF16)
        onehotT = [sb(f"onehotT{n}", [3 * EP, GT], BF16) for n in range(2)]
        offhotT = [sb(f"offhotT{n}", [3 * EP, GT], BF16) for n in range(2)]

        def psum(name, shape, dt=F32):
            return stack.enter_context(nc.psum_tensor(name, shape, dt))

        s_ps = psum("s_ps", [P, 2 * 512])
        st_ps = psum("st_ps", [P, 2 * 512])
        pv_ps = psum("pv_ps", [P, 512])
        t_ps = psum("t_ps", [P, 512])
        pp_ps = [psum(f"pp_ps{n}", [P, 512]) for n in range(2)]
        pv = pv_ps[:].rearrange("p (h d) -> p h d", h=H)
        attnT_ps = t_ps[:, 0:D]
        maxT_ps = t_ps[0:2 * HC, D:D + P // 2].bitcast(BF16)

        def y_ps(b):
            return pp_ps[b % 2][:, 0:D]

        s_small, s_w = sem("small_loaded"), sem("weights_loaded")
        s_const, s_wt, s_wtc = sem("constants"), sem("weight_transposed"), sem("weight_kept")
        s_b2z = sem("b2_cleared")
        s_set, s_pc = sem("dve_setup"), sem("pool_constant_step")
        ld_x, ld_c = [sem(f"x_loaded{n}") for n in range(2)], sem("ctx_loaded")
        st_x2 = [sem(f"x2_stored{n}") for n in range(2)]
        st_parts = [sem(f"{z}_parts_stored") for z in "qk"]
        pk = [[sem(f"{z}_packed_done{n}") for n in range(2)] for z in "qk"]
        s_bn, s_mv, s_ve, s_rstd, s_xn, s_xb = (sem(n) for n in (
            "bn_stats_done", "mean_var_done", "var_eps_done", "rstd_done", "xn_done", "xb_done"))
        s_pp, s_pe = sem("projection_in_psum"), sem("projection_kept")
        s_r, s_mid, s_lo = sem("remainder_done"), sem("mid_done"), sem("lo_done")
        s_s, s_red, s_hi, s_mp, s_mt, s_mte, s_st, s_exp, s_pv, s_rc, s_nrm = (sem(n) for n in (
            "scores_ready", "max_done", "max_hi_done", "max_parts_done", "max_transposed", "max_kept",
            "scoresT_ready", "exp_done", "pv_ready", "recip_done", "attn_normed"))
        s_uv, s_tpv = sem("pvT_kept"), sem("pv_transposed")
        s_at, s_ate = sem("attn_transposed"), sem("attnT_kept")
        s_y, s_x2 = sem("wo_ready"), sem("x2_done")

        CONSTS = 3 + E + 1 + 2 + 2 + 7
        SETUP_DVE = C + 8 + 4

        SLICES = [((1, 4), (1, 5)), ((1, 6), (1, 7)), (), ((1, 8),), (), ((1, 9),), ((2, 0), (2, 1)), ((2, 2), (2, 3))]
        MIDS = {0: 0, 1: 1}

        weight_banks = []
        for dst in (wqT, wkT, wvT, woT):
            weight_banks.append((dst[:].rearrange("p c d -> p (c d)"), C * D))
        weight_banks.append((cols[:], 3 * C + MC))
        weight_banks.append((ecols[:].rearrange("p c e -> p (c e)"), C * 3 * E))

        FIRST, LAST = 0, PAIRS - 1

        def pairs(engine, group_step):
            for n in range(2):
                group_step(FIRST, n, True, False)
            with engine.Fori(FIRST + 1, LAST) as pair:
                for n in range(2):
                    group_step(pair, n, False, False)
            for n in range(2):
                group_step(LAST, n, False, True)

        f_ld = [sem(f"ffn_x2_loaded{n}") for n in range(2)]
        f_st = [sem(f"ffn_out_stored{n}") for n in range(2)]
        (f_bn, f_mv, f_v1, f_r1, f_v2, f_v3, f_v4, f_r2, f_r12, f_xn) = (sem("ffn_" + n) for n in (
            "bn_stats", "mean_var", "var_eps", "rstd1", "var2a", "var2", "var2_eps", "rstd2", "rstd12", "xhat"))
        (f_tr, f_tre, f_g, f_gk, f_oh, f_ot, f_ote, f_h, f_he, f_y, f_out) = (sem("ffn_" + n) for n in (
            "xhatT_in_psum", "xhatT_kept", "logits_ready", "routing_step", "onehot_done", "onehotT_in_psum",
            "onehotT_kept", "hidden_in_psum", "hidden_kept", "out_in_psum", "out_done"))
        f_hh, f_hl, f_xh, f_xl, f_cp = (sem("ffn_" + n) for n in (
            "hidden_hi_done", "hidden_lo_done", "xhatT_hi_done", "xhatT_lo_done", "x2_copied"))
        f_gl, f_gle = sem("ffn_logitsT_in_psum"), sem("ffn_logitsT_kept")
        GK = 5
        tr_ps = pp_ps
        h_ps = [s_ps[:, 0:512], s_ps[:, 512:1024]]
        o_ps = [st_ps[:, 0:D], st_ps[:, 512:512 + D]]
        gT_ps = t_ps[:, 0:P]
        g_ps = t_ps[:, P:P + GB * EP].rearrange("p (b e) -> p b e", e=EP)[:, :, 0:E]
        onehotT_ps = pv_ps[0:3 * EP, 0:GT // 2].bitcast(BF16)

        def ffn_sync(sp):
            def load(pair, n):
                src = x2_v[index(sp, pair * 2 + n)]
                wait(sp, f_xn, at(pair, GB, n - 2, GB))
                wait(sp, f_cp, at(pair, 1, n - 2, 1))
                sp.dma_start(xin[n % 2][:], src).then_inc(f_ld[n % 2], 16)

            def store(pair, n):
                dst = out_v[index(sp, pair * 2 + n)]
                sp.wait_ge(f_out, at(pair, GB, n, GB))
                sp.dma_start(dst, xb[n % 2][:]).then_inc(f_st[n % 2], 16)

            load(0, 0)
            load(0, 1)

            def group(pair, n, is_first, is_last):
                if not is_last:
                    load(pair, n + 2)
                store(pair, n)

            pairs(sp, group)
            for n in range(2):
                sp.wait_ge(f_st[n], 16 * PAIRS)

        def ffn_pool(pool):
            g = nc.gpsimd

            def norm(pair, n):
                one = at(pair, 1, n, 1)
                pool.wait_ge(f_mv, at(pair, GB, n, GB))
                g.tensor_tensor(ve[:], mv[:, :, 1], eps[:], ALU.add).then_inc(f_v1, 1)
                pool.wait_ge(f_v1, one)
                g.tensor_tensor(rstd[:], ve[:], neg_half[:], ALU.pow).then_inc(f_r1, 1)
                pool.wait_ge(f_r1, one)
                g.tensor_tensor(ve[:], mv[:, :, 1], rstd[:], ALU.mult).then_inc(f_v2, 1)
                pool.wait_ge(f_v2, one)
                g.tensor_tensor(rstd2[:], ve[:], rstd[:], ALU.mult).then_inc(f_v3, 1)
                pool.wait_ge(f_v3, one)
                g.tensor_tensor(ve[:], rstd2[:], eps[:], ALU.add).then_inc(f_v4, 1)
                pool.wait_ge(f_v4, one)
                g.tensor_tensor(rstd2[:], ve[:], neg_half[:], ALU.pow).then_inc(f_r2, 1)
                pool.wait_ge(f_r2, one)
                g.tensor_tensor(rstd[:], rstd[:], rstd2[:], ALU.mult).then_inc(f_r12, 1)

            def lo_of_xT(pair, n):
                pool.wait_ge(f_xh, at(pair, C, n, C))
                g.tensor_tensor(xhT_lo[n % 2][:, 1, :].bitcast(F32R), xhT[n % 2][:, 1, :], xhT_hi[n % 2][:, 1, :],
                                ALU.subtract).then_inc(f_xl, 1)

            norm(0, 0)
            norm(0, 1)
            lo_of_xT(0, 0)

            def group(pair, n, is_first, is_last):
                more = not (is_last and n == 1)
                if not is_last:
                    norm(pair, n + 2)
                if more:
                    lo_of_xT(pair, n + 1)

            pairs(pool, group)

        def ffn_act(act):
            a = nc.scalar

            def keep_xT(pair, n, c):
                act.wait_ge(f_tr, at(pair, C, n, c + 1))
                a.copy(xhT[n % 2][:, c, :], tr_ps[c][:]).then_inc(f_tre, 1)

            def keep_onehot(pair, n):
                act.wait_ge(f_ot, at(pair, 1, n, 1))
                a.copy(onehotT[n % 2][:], onehotT_ps)
                a.activation(offhotT[n % 2][:], onehotT_ps, ACT.Copy, bias=-1.0).then_inc(f_ote, 1)

            def gelu(pair, n, m):
                act.wait_ge(f_h, at(pair, MC, n, m + 1))
                wait(act, f_hl, at(pair, MC, n - 1, m + 1))
                a.activation(hidden32[m], h_ps[m % 2], ACT.Gelu, bias=c1[:, m:m + 1]).then_inc(f_he, 1)

            def copy(pair, n):
                act.wait_ge(f_ld[n % 2], (pair + n // 2 + 1) * 16)
                wait(act, f_st[n % 2], (pair + n // 2) * 16)
                a.copy(xb[n % 2][:], xin[n % 2][:]).then_inc(f_cp, 1)

            copy(0, 0)
            for c in range(C):
                keep_xT(0, 0, c)

            def group(pair, n, is_first, is_last):
                keep_onehot(pair, n)
                for m in range(MC):
                    gelu(pair, n, m)
                    if m == 1 and not (is_last and n == 1):
                        copy(pair, n + 1)
                if not (is_last and n == 1):
                    for c in range(C):
                        keep_xT(pair, n + 1, c)

            pairs(act, group)

        def ffn_dve(dve):
            v = nc.vector

            def stats_of(pair, n):
                dve.wait_ge(f_ld[n % 2], (pair + n // 2 + 1) * 16)
                for b in range(GB):
                    v.bn_stats(stats[:, b, :], xin[n % 2][:, b, :]).then_inc(f_bn, 1)
                for b in range(GB):
                    count = in_register(dve, at(pair, GB, n, b + 1))
                    dve.wait_ge(s_const, 1)
                    dve.wait_ge(f_bn, count)
                    v.bn_aggr(mv[:, b, :], stats[:, b, :]).then_inc(f_mv, 1)

            def normalise(pair, n):
                dve.wait_ge(f_r12, at(pair, 1, n, 1))
                wait(dve, f_tr, at(pair, C, n - 1, C))
                for b in range(GB):
                    v.tensor_scalar(xn[:, b, :], xin[n % 2][:, b, :], mv[:, b, 0:1], rstd[:, b:b + 1],
                                    ALU.subtract, ALU.mult).then_inc(f_xn, 1)

            def route(pair, n):
                dve.wait_ge(f_g, at(pair, 1, n, 1))
                lg = g_ps
                topb = top[:].unsqueeze(2).broadcast_to([P, GB, E])
                v.tensor_reduce(top[:], lg, AX_X, ALU.max).then_inc(f_gk, 1)
                dve.wait_ge(f_gk, at(pair, GK, n, 1))
                v.tensor_tensor(hit[:], lg, topb, ALU.is_equal).then_inc(f_gk, 1)
                dve.wait_ge(f_gk, at(pair, GK, n, 2))
                v.tensor_tensor(first[:], hit[:], rank[:].unsqueeze(1).broadcast_to([P, GB, E]),
                                ALU.mult).then_inc(f_gk, 1)
                dve.wait_ge(f_gk, at(pair, GK, n, 3))
                v.tensor_reduce(top[:], first[:], AX_X, ALU.max).then_inc(f_gk, 1)
                dve.wait_ge(f_gk, at(pair, GK, n, 4))
                wait(dve, f_ot, at(pair, 1, n, 0))
                v.tensor_tensor(onehot[:, :, :, 0:E], first[:].unsqueeze(2).broadcast_to([P, GB, 3, E]),
                                top[:].unsqueeze(2).unsqueeze(3).broadcast_to([P, GB, 3, E]),
                                ALU.is_equal).then_inc(f_gk, 1)

            def keep_logits(pair, n):
                dve.wait_ge(f_gl, at(pair, 1, n, 1))
                v.tensor_copy(logitT[:], gT_ps).then_inc(f_gle, 1)

            def add(pair, n, b):
                dve.wait_ge(f_y, at(pair, GB, n, b + 1))
                if b == 0:
                    dve.wait_ge(f_cp, at(pair, 1, n, 1))
                xr = xb[n % 2][:, b, :]
                v.tensor_tensor(xr, xr, o_ps[b % 2], ALU.add).then_inc(f_out, 1)

            def split_hidden(pair, n, m):
                dve.wait_ge(f_he, at(pair, MC, n, m + 1))
                hi, lo = hT_hi[n % 2][:, m, :], hT_lo[n % 2][:, m, :]
                v.tensor_copy(hi.bitcast(F32R), hidden32[m]).then_inc(f_hh, 1)
                dve.wait_ge(f_hh, at(pair, MC, n, m + 1))
                v.tensor_tensor(lo.bitcast(F32R), hidden32[m], hi, ALU.subtract).then_inc(f_hl, 1)

            def split_xT(pair, n):
                for c in range(C):
                    dve.wait_ge(f_tre, at(pair, C, n, c + 1))
                    v.tensor_copy(xhT_hi[n % 2][:, c, :].bitcast(F32R), xhT[n % 2][:, c, :]).then_inc(f_xh, 1)
                dve.wait_ge(f_xh, at(pair, C, n, 1))
                v.tensor_tensor(xhT_lo[n % 2][:, 0, :].bitcast(F32R), xhT[n % 2][:, 0, :], xhT_hi[n % 2][:, 0, :],
                                ALU.subtract).then_inc(f_xl, 1)

            stats_of(0, 0)
            normalise(0, 0)
            stats_of(0, 1)
            split_xT(0, 0)
            keep_logits(0, 0)

            def group(pair, n, is_first, is_last):
                more = not (is_last and n == 1)
                route(pair, n)
                if more:
                    normalise(pair, n + 1)
                for m in range(MC):
                    split_hidden(pair, n, m)
                if not is_last:
                    stats_of(pair, n + 2)
                add(pair, n, 0)
                if more:
                    split_xT(pair, n + 1)
                add(pair, n, 1)
                if more:
                    keep_logits(pair, n + 1)
                add(pair, n, 2)
                add(pair, n, 3)

            pairs(dve, group)

        def ffn_pe(pe):
            t = nc.tensor

            def turn(pair, n, c):
                wait(pe, f_tre, at(pair, C, n - 1, c + 1))
                for b in range(GB):
                    if c == 0:
                        pe.wait_ge(f_xn, at(pair, GB, n, b + 1))
                    mm = t.transpose(tr_ps[c][:, b * T:(b + 1) * T], xn[:, b, c * P:(c + 1) * P], ident[:])
                mm.then_inc(f_tr, 1)

            def gate(pair, n):
                pe.wait_ge(f_tre, at(pair, C, n, C))
                wait(pe, f_gk, at(pair, GK, n, 0))
                for c in range(C):
                    for b in range(GB):
                        mm = t.matmul(gT_ps[b * EP:(b + 1) * EP, :], wg_pad[:, c, :], xhT[n % 2][:, c, b * T:(b + 1) * T],
                                      start=(c == 0), stop=(c == C - 1))
                mm.then_inc(f_gl, 1)

            def turn_logits(pair, n):
                pe.wait_ge(f_gle, at(pair, 1, n, 1))
                t.transpose(t_ps[:, P:2 * P], logitT[:], ident[:]).then_inc(f_g, 1)

            def turn_onehot(pair, n):
                pe.wait_ge(f_gk, at(pair, GK, n, GK))
                wait(pe, f_ote, at(pair, 1, n, 0))
                for b in range(GB):
                    mm = t.transpose(onehotT_ps[:, b * T:(b + 1) * T], onehot[:, b, :, :], ident_bf[:])
                mm.then_inc(f_ot, 1)

            def hidden(pair, n, m):
                wait(pe, f_he, at(pair, MC, n, m - 1))
                e = slice(EC * m, EC * (m + 1))
                if m == 0:
                    pe.wait_ge(f_xh, at(pair, C, n, C))
                for k, (w, x) in enumerate(((w1_hi, xhT_hi), (w1_lo, xhT_hi), (w1_hi, xhT_lo))):
                    if m == 0 and k == 2:
                        pe.wait_ge(f_xl, at(pair, C, n, C))
                    for c in range(C):
                        t.matmul(h_ps[m % 2], w[:, c, e, :].bitcast(F32R), x[n % 2][:, c, :].bitcast(F32R),
                                 start=(k == 0 and c == 0), stop=False)

            def mask(pair, n, m):
                if m == 0:
                    pe.wait_ge(f_ote, at(pair, 1, n, 1))
                t.matmul(h_ps[m % 2], far_sel[:, EC * m:EC * (m + 1), :], offhotT[n % 2][0:E, :],
                         start=False, stop=True).then_inc(f_h, 1)

            def output(pair, n, b):
                o = o_ps[b % 2]
                tok = slice(b * T, (b + 1) * T)
                wait(pe, f_out, at(pair, GB, n, b - 1))
                for m in range(MC):
                    if b == 0:
                        pe.wait_ge(f_hl, at(pair, MC, n, m + 1))
                    for k, (h, w) in enumerate(((hT_hi, w2_hi), (hT_hi, w2_lo), (hT_lo, w2_hi))):
                        t.matmul(o, h[n % 2][:, m, tok].bitcast(F32R), w[:, m, :].bitcast(F32R),
                                 start=(m == 0 and k == 0), stop=False)
                t.matmul(o, onehotT[n % 2][:, tok], b2p[:], start=False, stop=True).then_inc(f_y, 1)

            pe.wait_ge(s_x2, GROUPS * GB)
            for c in range(C):
                turn(0, 0, c)
            gate(0, 0)
            turn_logits(0, 0)

            def group(pair, n, is_first, is_last):
                more = not (is_last and n == 1)
                hidden(pair, n, 0)
                turn_onehot(pair, n)
                hidden(pair, n, 1)
                mask(pair, n, 0)
                mask(pair, n, 1)
                for m in range(2, MC):
                    hidden(pair, n, m)
                    mask(pair, n, m)
                if more:
                    for c in range(C):
                        turn(pair, n + 1, c)
                for b in range(GB):
                    output(pair, n, b)
                    if b == 1 and more:
                        gate(pair, n + 1)
                if more:
                    turn_logits(pair, n + 1)

            pairs(pe, group)

        block = stack.enter_context(nc.Block())

        @block.sync
        def _(sp):
            def load_x(pair, g):
                src = x_v[index(sp, pair * 2 + g)]
                wait(sp, s_xb, at(pair, 1, g - 2, 1))
                sp.dma_start(xin[g % 2][:], src).then_inc(ld_x[g % 2], 16)

            def load_c(pair, g):
                src = c_v[index(sp, pair * 2 + g)]
                wait(sp, s_pp, at(pair, ITEMS, g - 1, 2))
                sp.dma_start(cin[:], src).then_inc(ld_c, 16)

            def store_x2(pair, g):
                dst = x2_v[index(sp, pair * 2 + g)]
                wait(sp, s_x2, at(pair, GB, g, GB))
                sp.dma_start(dst, xb[g % 2][:]).then_inc(st_x2[g % 2], 16)

            def store_parts(pair, g, z):
                wait(sp, s_lo, at(pair, 2, g, z + 1))
                there = parts_dram[z][g % 2]
                sp.dma_start(there.rearrange("n (c p) t -> p n c t", p=P), parts[z][:]).then_inc(st_parts[z], 16)

            def pack(pair, g, z):
                there = parts_dram[z][g % 2]
                wait(sp, st_parts[z], at(pair, 16, g, 16))
                for n, part in enumerate((Q_PARTS, K_PARTS)[z]):
                    sp.dma_start(packed[z][g % 2][n * DH:(n + 1) * DH, :, :],
                                 there[part].rearrange("(h d) t -> d h t", d=DH)).then_inc(pk[z][g % 2], 16)

            for n, v in enumerate((bq, bk, bv)):
                sp.dma_start(rows[n * C:(n + 1) * C, :], v.rearrange("(c p) -> c p", p=P)).then_inc(s_small, 16)
            sp.dma_start(rows[3 * C:3 * C + MC, :], b1.rearrange("(m e) h -> m (e h)", e=EC)).then_inc(s_small, 16)
            for n, v in enumerate((wg, ln_s, ln_b)):
                sp.dma_start(erows[n * E:(n + 1) * E, :], v).then_inc(s_small, 16)
            sp.dma_start(bo_row[:], bo.rearrange("(a d) -> a d", a=1)).then_inc(s_small, 16)
            sp.wait_ge(s_b2z, 1)
            for k in range(3):
                sp.dma_start(b2f[k * EP:k * EP + E, :], b2).then_inc(s_small, 16)
            for v, t in ((wq, xn[:, 0:C, :]), (wk, xn[:, C:2 * C, :]),
                         (wv, z32[0][:, 0, :].rearrange("p (c d) -> p c d", c=C)),
                         (wo, z32[0][:, 1, :].rearrange("p (c d) -> p c d", c=C))):
                sp.dma_start(t, v.rearrange("(c p) d -> p c d", p=P)).then_inc(s_w, 16)
            for c in range(C):
                sp.dma_start(w1s[:, c, :, :], w1[:, c * P:(c + 1) * P, :].rearrange("e p h -> p e h")).then_inc(s_w, 16)
            sp.dma_start(w2s, w2.rearrange("e h d -> (e h) d").rearrange("(m p) d -> p m d", p=P)).then_inc(s_w, 16)

            load_x(0, 0)
            load_c(0, 0)
            load_x(0, 1)
            load_c(0, 1)
            for z in range(2):
                store_parts(0, 0, z)
                pack(0, 0, z)

            def group(pair, g, is_first, is_last):
                more = not (is_last and g == 1)
                if not is_last:
                    load_x(pair, g + 2)
                    load_c(pair, g + 2)
                if more:
                    for z in range(2):
                        store_parts(pair, g + 1, z)
                        pack(pair, g + 1, z)
                if not (is_first and g == 0):
                    store_x2(pair, g - 1)

            pairs(sp, group)
            store_x2(LAST, 1)
            for n in range(2):
                sp.wait_ge(st_x2[n], 16 * PAIRS)
            ffn_sync(sp)

        @block.gpsimd
        def _(pool):
            g = nc.gpsimd
            g.memset(ident[:], 0.0).then_inc(s_pc, 1)
            g.memset(head_sel[:], 0.0).then_inc(s_pc, 1)
            g.memset(far_sel[:], 0.0).then_inc(s_pc, 1)
            g.memset(neg_half[:], -0.5).then_inc(s_const, 1)
            g.memset(eps[:], EPS).then_inc(s_const, 1)
            g.memset(ones_row[:], 1.0).then_inc(s_const, 1)
            for e in range(E):
                g.memset(rank[:, e:e + 1], float(E - e)).then_inc(s_const, 1)
            pool.wait_ge(s_pc, 3)
            g.affine_select(out=ident[:], in_=ident[:], compare_op=ALU.not_equal, fill=1.0, base=0,
                            pattern=[[-1, P]], channel_multiplier=1).then_inc(s_pc, 1)
            g.affine_select(out=head_sel[:], in_=head_sel[:], compare_op=ALU.not_equal, fill=1.0, base=0,
                            pattern=[[-1, HC], [0, P]], channel_multiplier=1).then_inc(s_pc, 1)
            g.affine_select(out=far_sel[:], in_=far_sel[:], compare_op=ALU.not_equal, fill=-FAR, base=0,
                            pattern=[[-1, MC * EC], [0, HID]], channel_multiplier=1).then_inc(s_const, 1)
            for n in range(2):
                g.memset(v1[n][:], 1.0).then_inc(s_const, 1)
            pool.wait_ge(s_pc, 5)
            g.affine_select(out=head_sel[:], in_=head_sel[:], compare_op=ALU.not_equal, fill=1.0, base=-HC,
                            pattern=[[-1, HC], [0, P]], channel_multiplier=1).then_inc(s_const, 1)
            g.tensor_copy(ident_bf[:], ident[:]).then_inc(s_const, 1)

            def norm(pair, n):
                pool.wait_ge(s_mv, at(pair, GB, n, GB))
                g.tensor_tensor(ve[:], mv[:, :, 1], eps[:], ALU.add).then_inc(s_ve, 1)
                pool.wait_ge(s_ve, at(pair, 1, n, 1))
                g.tensor_tensor(rstd[:], ve[:], neg_half[:], ALU.pow).then_inc(s_rstd, 1)

            def residual(pair, n):
                pool.wait_ge(s_xn, at(pair, GB, n, GB))
                wait(pool, st_x2[n % 2], (pair + n // 2) * 16)
                for b in range(GB):
                    last = g.tensor_tensor(xb[n % 2][:, b, :], xin[n % 2][:, b, :], bo_all[:], ALU.add)
                last.then_inc(s_xb, 1)

            norm(0, 0)
            pool.wait_ge(s_set, SETUP_DVE)
            residual(0, 0)
            norm(0, 1)

            def group(pair, n, is_first, is_last):
                if not is_last:
                    norm(pair, n + 2)
                if not (is_last and n == 1):
                    residual(pair, n + 1)

            pairs(pool, group)
            ffn_pool(pool)

        @block.scalar
        def _(act):
            a = nc.scalar

            def keep_max(pair, n, u):
                act.wait_ge(s_mt, at(pair, UNITS, n, u + 1))
                a.copy(negmaxT[u % 2][0:2 * HC, :], maxT_ps).then_inc(s_mte, 1)

            def keep_pvT(pair, n, b):
                act.wait_ge(s_pv, at(pair, UNITS, n, C * (b + 1)))
                wait(act, s_tpv, at(pair, GB, n, b))
                a.copy(uvT[:], pv_ps[:]).then_inc(s_uv, 1)

            def item(pair, n, k):
                act.wait_ge(s_pp, at(pair, ITEMS, n, k + 1))
                ps = pp_ps[k % 2]
                if k < 4:
                    last = a.copy((cT, xT)[k // 2][:, k % 2, :], ps[:])
                elif k < 8:
                    z, m = (k - 4) // 2, k % 2
                    if m == 0:
                        wait(act, s_lo, at(pair, 2, n - 1, z + 1))
                        wait(act, st_parts[z], at(pair, 16, n - 1, 16))
                    bias = cols[:, z * C + m:z * C + m + 1]
                    a.activation(z32[z][:, m, :], ps[:], ACT.Identity, bias=bias)
                    last = a.activation(parts[z][:, 0, m, :], ps[:], ACT.Identity, bias=bias)
                else:
                    b = 2 * (k - 8)
                    last = a.copy(v1[n % 2][:, b:b + 2, :, 0:DH],
                                  ps[:].rearrange("p (b h d) -> p b h d", b=2, d=DH))
                last.then_inc(s_pe, 1)

            def mid(pair, n, z):
                act.wait_ge(s_r, at(pair, 2, n, z + 1))
                a.copy(parts[z][:, 1, :, :], z32[z][:]).then_inc(s_mid, 1)

            def exp(pair, n, u):
                act.wait_ge(s_st, at(pair, UNITS, n, u + 1))
                wait(act, s_pv, at(pair, UNITS, n, u - 1))
                a.activation(pT[u % 2][:], st_ps[:], ACT.Exp, scale=DH ** -0.5).then_inc(s_exp, 1)

            def items(pair, n, u, is_last):
                for ahead, k in SLICES[u]:
                    if not is_last or n + ahead < 2:
                        item(pair, n + ahead, k)

            for k, (dst, width) in enumerate(weight_banks):
                act.wait_ge(s_wt, k + 1)
                a.copy(dst, pp_ps[k % 2][0:P, 0:width]).then_inc(s_wtc, 1)
            act.wait_ge(s_set, SETUP_DVE)

            for k in range(ITEMS):
                item(0, 0, k)
                if k == 8:
                    mid(0, 0, 0)
            mid(0, 0, 1)
            for k in range(4):
                item(0, 1, k)

            def group(pair, n, is_first, is_last):
                more = not (is_last and n == 1)
                for u in range(UNITS):
                    keep_max(pair, n, u)
                    if u % 2 == 1:
                        if u > 1:
                            keep_pvT(pair, n, u // 2 - 1)
                        elif not (is_first and n == 0):
                            keep_pvT(pair, n - 1, GB - 1)
                    if u > 1:
                        exp(pair, n, u)
                    items(pair, n, u, is_last)
                    if u <= 1:
                        exp(pair, n, u)
                    if more and u in MIDS:
                        mid(pair, n + 1, MIDS[u])

            pairs(act, group)
            keep_pvT(LAST, 1, GB - 1)
            ffn_act(act)

        @block.vector
        def _(dve):
            v = nc.vector
            step = [0]

            def setup(ins):
                step[0] += 1
                ins.then_inc(s_set, 1)
                dve.wait_ge(s_set, step[0])

            def stats_of(pair, n):
                dve.wait_ge(ld_x[n % 2], (pair + n // 2 + 1) * 16)
                for b in range(GB):
                    v.bn_stats(stats[:, b, :], xin[n % 2][:, b, :]).then_inc(s_bn, 1)
                for b in range(GB):
                    count = in_register(dve, at(pair, GB, n, b + 1))
                    dve.wait_ge(s_const, 1)
                    dve.wait_ge(s_bn, count)
                    v.bn_aggr(mv[:, b, :], stats[:, b, :]).then_inc(s_mv, 1)

            def normalise(pair, n):
                dve.wait_ge(s_rstd, at(pair, 1, n, 1))
                wait(dve, s_pp, at(pair, ITEMS, n - 1, 4))
                for b in range(GB):
                    v.tensor_scalar(xn[:, b, :], xin[n % 2][:, b, :], mv[:, b, 0:1], rstd[:, b:b + 1],
                                    ALU.subtract, ALU.mult).then_inc(s_xn, 1)

            def remainder(pair, n, z):
                dve.wait_ge(s_pe, at(pair, ITEMS, n, 6 + 2 * z))
                v.tensor_tensor(z32[z][:], z32[z][:], parts[z][:, 0, :, :], ALU.subtract).then_inc(s_r, 1)

            def lo(pair, n, z):
                dve.wait_ge(s_mid, at(pair, 2, n, z + 1))
                v.tensor_tensor(parts[z][:, 2, :, :], z32[z][:], parts[z][:, 1, :, :],
                                ALU.subtract).then_inc(s_lo, 1)

            def maxima(pair, n, u):
                dve.wait_ge(s_s, at(pair, UNITS, n, u + 1))
                v.tensor_reduce(negmax[u % 2][:], s_ps[:].rearrange("p (h s) -> p h s", s=P), AX_X, ALU.max,
                                negate=True).then_inc(s_red, 1)
                dve.wait_ge(s_red, at(pair, UNITS, n, u + 1))
                wait(dve, s_mt, at(pair, UNITS, n, u - 1))
                v.tensor_copy(negmax_p[u % 2][:, 0:HC], negmax[u % 2][:]).then_inc(s_hi, 1)
                dve.wait_ge(s_hi, at(pair, UNITS, n, u + 1))
                v.tensor_tensor(negmax_p[u % 2][:, HC:2 * HC], negmax[u % 2][:], negmax_p[u % 2][:, 0:HC],
                                ALU.subtract).then_inc(s_mp, 1)

            def norm(pair, n, b):
                dve.wait_ge(s_tpv, at(pair, GB, n, b + 1))
                v.reciprocal(recip[:], pv[:, :, DH]).then_inc(s_rc, 1)
                dve.wait_ge(s_rc, at(pair, GB, n, b + 1))
                wait(dve, s_at, at(pair, GB, n, b))
                v.tensor_tensor(attn[:], pv[:, :, 0:DH], recip[:].unsqueeze(2).broadcast_to([P, H, DH]),
                                ALU.mult).then_inc(s_nrm, 1)

            def keep_attn(pair, n, b):
                dve.wait_ge(s_at, at(pair, GB, n, b + 1))
                wait(dve, s_y, at(pair, GB, n, b - 1))
                v.tensor_copy(aT[b % 2][:], attnT_ps.rearrange("p (c t) -> p c t", c=C)).then_inc(s_ate, 1)

            def residual(pair, n, b):
                dve.wait_ge(s_y, at(pair, GB, n, b + 1))
                if b == 0:
                    dve.wait_ge(s_xb, at(pair, 1, n, 1))
                xr = xb[n % 2][:, b, :]
                v.tensor_tensor(xr, xr, y_ps(b), ALU.add).then_inc(s_x2, 1)

            v.memset(b2f[:], 0.0).then_inc(s_b2z, 1)
            v.memset(onehot[:].rearrange("p b k e -> p (b k e)"), 0.0).then_inc(s_const, 1)
            for z in range(2):
                for n in range(2):
                    v.memset(packed[z][n][KP:P, :, :].rearrange("p h t -> p (h t)"), 0.0).then_inc(s_const, 1)
            for n in range(2):
                v.memset(negmaxT[n][:].bitcast(F32), 0.0).then_inc(s_const, 1)
            stats_of(0, 0)
            dve.wait_ge(s_wt, len(weight_banks) + 1)
            dve.wait_ge(s_wtc, len(weight_banks))
            for m in range(MC):
                for e in range(EC):
                    r = slice(e * HID, (e + 1) * HID)
                    v.tensor_tensor(c1[r, m:m + 1], pp_ps[0][r, EC * m + e:EC * m + e + 1],
                                    cols[r, 3 * C + m:3 * C + m + 1], ALU.add)
            for c in range(C):
                ls = ecols[:, c, E:2 * E].unsqueeze(2).broadcast_to([P, E, HID])
                setup(v.tensor_tensor(w1s[:, c, :, :], w1s[:, c, :, :], ls, ALU.mult))
            for full, upper, rest in ((w1s.rearrange("p c e h -> p (c e h)"), w1_hi[:].rearrange("p c e h -> p (c e h)"),
                                  w1_lo[:].rearrange("p c e h -> p (c e h)")),
                                 (w2s.rearrange("p m d -> p (m d)"), w2_hi[:].rearrange("p m d -> p (m d)"),
                                  w2_lo[:].rearrange("p m d -> p (m d)"))):
                setup(v.tensor_copy(upper.bitcast(F32R), full))
                setup(v.tensor_tensor(rest.bitcast(F32R), full, upper, ALU.subtract))
            setup(v.memset(wg_pad[:].rearrange("p c e -> p (c e)"), 0.0))
            setup(v.tensor_copy(wg_pad[:, :, 0:E], ecols[:, :, 0:E]))
            setup(v.tensor_copy(b2p[:], b2f[:]))
            setup(v.tensor_tensor(b2r[:], b2f[:], b2p[:], ALU.subtract))
            for k in (1, 2):
                setup(v.tensor_copy(b2p[k * EP:(k + 1) * EP, :], b2r[k * EP:(k + 1) * EP, :]))
            r = slice(2 * EP, 3 * EP)
            setup(v.tensor_tensor(b2p[r, :], b2r[r, :], b2p[r, :], ALU.subtract))
            dve.wait_ge(s_wt, len(weight_banks) + 2)
            setup(v.tensor_copy(bo_all[:], pp_ps[1][:, 0:D]))

            normalise(0, 0)
            remainder(0, 0, 0)
            remainder(0, 0, 1)
            lo(0, 0, 0)
            lo(0, 0, 1)
            stats_of(0, 1)
            normalise(0, 1)
            maxima(0, 0, 0)

            def group(pair, n, is_first, is_last):
                more = not (is_last and n == 1)
                for u in range(UNITS):
                    if u % 2 == 0:
                        if u > 2:
                            residual(pair, n, u // 2 - 2)
                        elif not (is_first and n == 0):
                            residual(pair, n - 1, GB - 2 + u // 2)
                    if u + 1 < UNITS:
                        maxima(pair, n, u + 1)
                    elif more:
                        maxima(pair, n + 1, 0)
                    if more and u == 0:
                        remainder(pair, n + 1, 0)
                    if more and u == 2:
                        lo(pair, n + 1, 1)
                    if u % 2 == 1:
                        done = (n, u // 2 - 1) if u > 1 else (n - 1, GB - 1)
                        there = u > 1 or not (is_first and n == 0)
                        if more and u == 1:
                            lo(pair, n + 1, 0)
                        if there:
                            norm(pair, *done)
                            keep_attn(pair, *done)
                        if more and u == 1:
                            remainder(pair, n + 1, 1)
                    if not is_last:
                        if u == 3:
                            stats_of(pair, n + 2)
                        if u == 5:
                            normalise(pair, n + 2)

            pairs(dve, group)
            residual(LAST, 1, GB - 2)
            norm(LAST, 1, GB - 1)
            keep_attn(LAST, 1, GB - 1)
            residual(LAST, 1, GB - 1)
            ffn_dve(dve)

        @block.tensor
        def _(pe):
            t = nc.tensor

            def scores(pair, n, u):
                b, m = u // C, u % C
                tok = slice(b * T, (b + 1) * T)
                if u == 0:
                    for z in range(2):
                        pe.wait_ge(pk[z][n % 2], (pair + n // 2 + 1) * PACK)
                wait(pe, s_red, at(pair, UNITS, n, u))
                for j in range(HC):
                    h = m * HC + j
                    mm = t.matmul(s_ps[:, j * P:(j + 1) * P], packed[0][n % 2][:, h, tok],
                                  packed[1][n % 2][:, h, tok], start=True, stop=True)
                mm.then_inc(s_s, 1)

            def turn_max(pair, n, u):
                pe.wait_ge(s_mp, at(pair, UNITS, n, u + 1))
                if u % 2 == 0:
                    wait(pe, s_ate, at(pair, GB, n, u // 2 - 1))
                t.transpose(maxT_ps, negmax_p[u % 2][:], ident_bf[:]).then_inc(s_mt, 1)

            def turn_attn(pair, n, b):
                pe.wait_ge(s_nrm, at(pair, GB, n, b + 1))
                for c in range(C):
                    mm = t.transpose(attnT_ps[:, c * P:(c + 1) * P], attn[:, c * HC:(c + 1) * HC, :], ident[:])
                mm.then_inc(s_at, 1)

            def scoresT(pair, n, u):
                b, m = u // C, u % C
                tok = slice(b * T, (b + 1) * T)
                pe.wait_ge(s_mte, at(pair, UNITS, n, u + 1))
                wait(pe, s_exp, at(pair, UNITS, n, u))
                for j in range(HC):
                    h = m * HC + j
                    o = st_ps[:, j * P:(j + 1) * P]
                    t.matmul(o, packed[1][n % 2][:, h, tok], packed[0][n % 2][:, h, tok],
                             start=True, stop=False)
                    mm = t.matmul(o, head_sel[:, j, :], negmaxT[u % 2][:], start=False, stop=True)
                mm.then_inc(s_st, 1)

            def values(pair, n, u):
                b, m = u // C, u % C
                pe.wait_ge(s_exp, at(pair, UNITS, n, u + 1))
                if m == 0:
                    wait(pe, s_nrm, at(pair, GB, n, b))
                if u == 0:
                    pe.wait_ge(s_pe, at(pair, ITEMS, n, ITEMS))
                for j in range(HC):
                    h = m * HC + j
                    strip, block = h % 4 * HP, h // 4 * P
                    mm = t.matmul(pv_ps[strip:strip + HP, block:block + P], v1[n % 2][:, b, h, :],
                                  pT[u % 2][:, j * P:(j + 1) * P], start=True, stop=True)
                mm.then_inc(s_pv, 1)

            def turn_pv(pair, n, b):
                pe.wait_ge(s_uv, at(pair, GB, n, b + 1))
                for k in range(4):
                    mm = t.transpose(pv_ps[:, k * P:(k + 1) * P], uvT[:, k * P:(k + 1) * P], ident[:])
                mm.then_inc(s_tpv, 1)

            def project_out(pair, n, b, now, keeps):
                pe.wait_ge(s_ate, at(pair, GB, n, b + 1))
                if keeps:
                    pe.wait_ge(s_pe, at(pair, ITEMS, now + 1, keeps))
                wait(pe, s_x2, at(pair, GB, n, b - 1))
                for c in range(C):
                    mm = t.matmul(y_ps(b), aT[b % 2][:, c, :], woT[:, c, :], start=(c == 0), stop=(c == C - 1))
                mm.then_inc(s_y, 1)

            def item(pair, n, k):
                ps = pp_ps[k % 2]
                if k == 0:
                    pe.wait_ge(ld_c, at(pair, 16, n, 16))
                if k == 2:
                    pe.wait_ge(s_xn, at(pair, GB, n, GB))
                wait(pe, s_pe, at(pair, ITEMS, n, k if k == 4 else k - 1))
                if k in (0, 1):
                    wait(pe, s_x2, at(pair, GB, n - 2, k + 1))
                if k == 4:
                    wait(pe, s_x2, at(pair, GB, n - 2, 3))
                if k == 9:
                    wait(pe, s_x2, at(pair, GB, n - 2, 4))
                if k < 4:
                    for b in range(GB):
                        mm = t.transpose(ps[:, b * T:(b + 1) * T],
                                         (cin, xn)[k // 2][:, b, k % 2 * P:(k % 2 + 1) * P], ident[:])
                elif k < 8:
                    w, src = ((wqT, xT), (wkT, cT))[(k - 4) // 2]
                    for c in range(C):
                        mm = t.matmul(ps[:], w[:, c, k % 2 * P:(k % 2 + 1) * P], src[:, c, :],
                                      start=(c == 0), stop=(c == C - 1))
                else:
                    for b in range(2):
                        tok = (2 * (k - 8) + b) * T
                        for c in range(C):
                            mm = t.matmul(ps[:, b * D:(b + 1) * D], cT[:, c, tok:tok + T], wvT[:, c, :],
                                          start=(c == 0), stop=(c == C - 1))
                mm.then_inc(s_pp, 1)

            def items(pair, n, u, is_last):
                for ahead, k in SLICES[u]:
                    if not is_last or n + ahead < 2:
                        item(pair, n + ahead, k)

            pe.wait_ge(s_const, CONSTS)
            pe.wait_ge(s_small, 16 * 11)
            pe.wait_ge(s_w, 16 * 7)
            sources = [xn[:, 0:C, :], xn[:, C:2 * C, :], z32[0][:, 0, :].rearrange("p (c d) -> p c d", c=C),
                       z32[0][:, 1, :].rearrange("p (c d) -> p c d", c=C)]
            for k, w in enumerate(sources):
                if k >= 2:
                    pe.wait_ge(s_wtc, k - 1)
                for ci in range(C):
                    for co in range(C):
                        mm = t.transpose(pp_ps[k % 2][:, ci * D + co * P:ci * D + (co + 1) * P],
                                         w[:, co, ci * P:(ci + 1) * P], ident[:])
                mm.then_inc(s_wt, 1)
            pe.wait_ge(s_wtc, 3)
            NR = 3 * C + MC
            t.transpose(pp_ps[0][:, 0:NR], rows[:], ident[0:NR, 0:NR]).then_inc(s_wt, 1)
            pe.wait_ge(s_wtc, 4)
            for c in range(C):
                mm = t.transpose(pp_ps[1][:, c * 3 * E:(c + 1) * 3 * E], erows[:, c * P:(c + 1) * P],
                                 ident[0:3 * E, 0:3 * E])
            mm.then_inc(s_wt, 1)
            pe.wait_ge(s_wtc, 6)
            for m in range(MC):
                for c in range(C):
                    mm = t.matmul(pp_ps[0][:, EC * m:EC * (m + 1)], w1s[:, c, EC * m:EC * (m + 1), :],
                                  ecols[:, c, 2 * E + EC * m:2 * E + EC * (m + 1)], start=(c == 0), stop=(c == C - 1))
            mm.then_inc(s_wt, 1)
            for c in range(C):
                t.matmul(pp_ps[1][:, 0:D], cols[:, 2 * C + c:2 * C + c + 1].broadcast_to([P, P]), woT[:, c, :],
                         start=(c == 0), stop=False)
            t.matmul(pp_ps[1][:, 0:D], ones_row[:], bo_row[:], start=False, stop=True).then_inc(s_wt, 1)
            pe.wait_ge(s_set, SETUP_DVE)

            for k in range(ITEMS):
                item(0, 0, k)
            for k in range(4):
                item(0, 1, k)
            scores(0, 0, 0)

            def group(pair, n, is_first, is_last):
                more = not (is_last and n == 1)
                for u in range(UNITS):
                    done = (n, u // 2 - 1) if u > 1 else (n - 1, GB - 1)
                    there = u % 2 == 1 and (u > 1 or not (is_first and n == 0))
                    turn_max(pair, n, u)
                    if u + 1 < UNITS:
                        scores(pair, n, u + 1)
                    elif more:
                        scores(pair, n + 1, 0)
                    if u <= 1:
                        items(pair, n, u, is_last)
                        if there:
                            turn_pv(pair, *done)
                        scoresT(pair, n, u)
                    else:
                        scoresT(pair, n, u)
                        if there:
                            turn_pv(pair, *done)
                        items(pair, n, u, is_last)
                    if there:
                        turn_attn(pair, *done)
                    if u > 0:
                        values(pair, n, u - 1)
                    elif not (is_first and n == 0):
                        values(pair, n - 1, UNITS - 1)
                    if there:
                        keeps = {1: 8, 3: 9, 5: 10, 7: 10 if is_last else 13}[u] if more else 0
                        project_out(pair, *done, n, keeps)

            pairs(pe, group)
            values(LAST, 1, UNITS - 1)
            turn_pv(LAST, 1, GB - 1)
            turn_attn(LAST, 1, GB - 1)
            project_out(LAST, 1, GB - 1, 2, 0)
            ffn_pe(pe)


_INS = ['x', 'ctx_1024'] + ['L0_xattn_' + n for n in ('wq_w', 'wq_b', 'wk_w', 'wk_b', 'wv_w', 'wv_b', 'wo_w', 'wo_b')] + \
    ['L0_ffn_' + n for n in ('Wg', 'ln_scale', 'ln_bias', 'W1', 'b1', 'W2', 'b2')]


def kernel(**inputs):
    import numpy as _np
    import concourse.bacc as _bacc
    from concourse import mybir as _mybir
    from concourse.bass_utils import run_bass_kernel_spmd as _run

    nc = _bacc.Bacc("TRN2", target_bir_lowering=False, num_devices=1)
    arrays, args = {}, []
    for name in _INS:
        a = _np.ascontiguousarray(inputs[name])
        arrays[f"in_{name}_dram"] = a
        args.append(nc.dram_tensor(f"in_{name}_dram", a.shape, _mybir.dt.from_np(a.dtype), kind="ExternalInput").ap())
    shape = inputs["x"].shape
    args.append(nc.dram_tensor("out_0_dram", shape, _mybir.dt.float32, kind="ExternalOutput").ap())
    xattn_moe(nc, *args)
    r = _run(nc, [arrays], core_ids=[0])
    return r.results[0]["out_0_dram"]
```

```python
from contextlib import ExitStack

import concourse.bass as bass
from concourse import mybir

F32 = mybir.dt.float32
F32R = mybir.dt.float32r
BF16 = mybir.dt.bfloat16
ALU = mybir.AluOpType
ACT = mybir.ActivationFunctionType
AX_X = mybir.AxisListType.X

P = 128
EPS = 1e-5
FAR = -float(2**30)


def at(pair, per_group, group, k):
    return pair * (2 * per_group) + (group * per_group + k)


def wait(engine, semaphore, value):
    if not isinstance(value, int) or value > 0:
        engine.wait_ge(semaphore, value)


def index(engine, value):
    return value if isinstance(value, int) else engine.snap(value)


def in_register(engine, value):
    return value if isinstance(value, int) else engine.to_reg(value)


def xattn_moe(nc, x, ctx_in, wq, bq, wk, bk, wv, bv, wo, bo, wg, ln_s, ln_b, w1, b1, w2, b2, out):
    BATCH, T, D = x.shape
    E, _, HID = w1.shape
    DH = 16
    H = D // DH
    C = D // P
    HC = H // C
    GB = 4
    GT = GB * T
    GROUPS = BATCH // GB
    PAIRS = GROUPS // 2
    UNITS = GB * C
    MC = E * HID // P
    EC = P // HID
    assert T == P and D == 256 and GROUPS % 2 == 0 and PAIRS > 2 and GROUPS * GB == BATCH

    Q_PARTS = (0, 0, 0, 1, 1, 2)
    K_PARTS = (0, 1, 2, 0, 1, 0)
    NPROD = len(Q_PARTS)
    KP = NPROD * DH
    PACK = 16 * NPROD
    EP = 32
    HP = 2 * DH
    ITEMS = 10

    x_v = x.rearrange("(g b) t d -> g t b d", b=GB)
    c_v = ctx_in.rearrange("(g b) t d -> g t b d", b=GB)
    out_v = out.rearrange("(g b) t d -> g t b d", b=GB)
    parts_dram = [[nc.dram_tensor(f"{z}_parts_scratch{n}", [3, D, GT], BF16, kind="Internal").ap()
                   for n in range(2)] for z in "qk"]
    x2_dram = nc.dram_tensor("x2_scratch", [BATCH, T, D], F32, kind="Internal").ap()
    x2_v = x2_dram.rearrange("(g b) t d -> g t b d", b=GB)

    with ExitStack() as stack:
        def sb(name, shape, dt=F32):
            return stack.enter_context(nc.sbuf_tensor(name, shape, dt))

        def sem(name):
            return stack.enter_context(nc.semaphore(name))

        ident = sb("ident", [P, P])
        ident_bf = sb("ident_bf", [P, P], BF16)
        ones_row = sb("ones_row", [1, P])
        head_sel = sb("head_sel", [P, HC, P], BF16)
        far_sel = sb("far_sel", [E, MC * EC, HID], BF16)
        wqT, wkT, wvT, woT = ([sb(n + part, [P, C, D]) for part in ("_hi", "_lo")] for n in ("wqT", "wkT", "wvT", "woT"))
        w1_hi, w1_lo = (sb(n, [P, C, E, HID]) for n in ("w1_hi", "w1_lo"))
        w2_hi, w2_lo = (sb(n, [P, MC, D]) for n in ("w2_hi", "w2_lo"))
        rows = sb("rows", [3 * C + MC, P])
        cols = sb("cols", [P, 3 * C + MC])
        erows = sb("erows", [3 * E, D])
        ecols = sb("ecols", [P, C, 3 * E])
        wg_pad = sb("wg_pad", [P, C, EP])
        c1 = sb("c1", [P, MC])
        bo_row = sb("bo_row", [1, D])
        bo_all = sb("bo_all", [P, D])
        b2f = sb("b2f", [3 * EP, D])
        b2r = sb("b2r", [3 * EP, D])
        b2p = sb("b2p", [3 * EP, D], BF16)
        rank = sb("rank", [P, E])

        xin = [sb(f"xin{n}", [P, GB, D]) for n in range(2)]
        cin = sb("cin", [P, GB, D])
        stats = sb("stats", [P, GB, 6])
        mv = sb("mv", [P, GB, 2])
        ve = sb("ve", [P, GB])
        rstd = sb("rstd", [P, GB])
        rstd2 = sb("rstd2", [P, GB])
        neg_half = sb("neg_half", [P, GB])
        eps = sb("eps", [P, GB])
        xn = sb("xn", [P, GB, D])
        xT = [sb("xT" + part, [P, C, GT]) for part in ("_hi", "_lo")]
        cT = [sb("cT" + part, [P, C, GT]) for part in ("_hi", "_lo")]
        z32 = [sb("q32", [P, C, GT]), sb("k32", [P, C, GT])]
        parts = [sb("q_parts", [P, 3, C, GT], BF16), sb("k_parts", [P, 3, C, GT], BF16)]
        packed = [[sb(f"{z}_packed{n}", [P, H, GT], BF16) for n in range(2)] for z in "qk"]
        v1 = [sb(f"v{n}", [P, GB, H, HP]) for n in range(2)]
        xb = [sb(f"xb{n}", [P, GB, D]) for n in range(2)]
        negmax = [sb(f"negmax{n}", [P, HC]) for n in range(2)]
        negmax_p = [sb(f"negmax_p{n}", [P, 2 * HC], BF16) for n in range(2)]
        negmaxT = [sb(f"negmaxT{n}", [P, P], BF16) for n in range(2)]
        pT = [sb(f"pT{n}", [P, HC * P]) for n in range(2)]
        w1s = pT[1][:].rearrange("p (c e h) -> p c e h", c=C, e=E)
        w2s = pT[0][:].rearrange("p (m d) -> p m d", m=MC)
        recip = sb("recip", [P, H])
        uvT = sb("uvT", [P, 512])
        attn = sb("attn", [P, H, DH])
        aT = [[sb(f"aT{n}{part}", [P, C, P]) for part in ("_hi", "_lo")] for n in range(2)]
        SPLIT = ((0, 0), (0, 1), (1, 0))

        def rows_of(packed_n):
            return packed_n[:, :, :].rearrange("p h t -> p (h t)").bitcast(F32).rearrange("p (m t) -> p m t", t=GT)

        hT_hi, hT_lo = ([rows_of(packed[0][n])[:, k * MC:(k + 1) * MC, :] for n in range(2)] for k in range(2))
        xhT_hi, xhT_lo = ([rows_of(packed[1][n])[:, k * C:(k + 1) * C, :] for n in range(2)] for k in range(2))
        xhT = z32
        hidden32 = [pT[m // 2][:, m % 2 * GT:(m % 2 + 1) * GT] for m in range(MC)]
        logitT = sb("logitT", [P, P])
        top = sb("top", [P, GB])
        hit = sb("hit", [P, GB, E])
        first = sb("first", [P, GB, E])
        onehot = sb("onehot", [P, GB, 3, EP], BF16)
        onehotT = [sb(f"onehotT{n}", [3 * EP, GT], BF16) for n in range(2)]
        offhotT = [sb(f"offhotT{n}", [3 * EP, GT], BF16) for n in range(2)]

        def psum(name, shape, dt=F32):
            return stack.enter_context(nc.psum_tensor(name, shape, dt))

        s_ps = psum("s_ps", [P, 2 * 512])
        st_ps = psum("st_ps", [P, 2 * 512])
        pv_ps = psum("pv_ps", [P, 512])
        t_ps = psum("t_ps", [P, 512])
        pp_ps = [psum(f"pp_ps{n}", [P, 512]) for n in range(2)]
        pv = pv_ps[:].rearrange("p (h d) -> p h d", h=H)
        attnT_ps = t_ps[:, 0:D]
        maxT_ps = t_ps[0:2 * HC, D:D + P // 2].bitcast(BF16)

        def y_ps(b):
            return pp_ps[(b + 1) % 2][:, 0:D]

        s_small, s_w, s_wf = sem("small_loaded"), sem("weights_loaded"), sem("ffn_weights_loaded")
        s_const, s_wt, s_wtc = sem("constants"), sem("weight_transposed"), sem("weight_kept")
        s_b2z, s_wl, s_pad, s_bo = (sem(n) for n in ("b2_cleared", "weight_lo_done", "pad_rows_cleared", "bo_kept"))
        s_set, s_pc = sem("dve_setup"), sem("pool_constant_step")
        ld_x, ld_c = [sem(f"x_loaded{n}") for n in range(2)], sem("ctx_loaded")
        st_x2 = [sem(f"x2_stored{n}") for n in range(2)]
        st_parts = [sem(f"{z}_parts_stored") for z in "qk"]
        pk = [[sem(f"{z}_packed_done{n}") for n in range(2)] for z in "qk"]
        s_bn, s_mv, s_ve, s_rstd, s_xn, s_xb = (sem(n) for n in (
            "bn_stats_done", "mean_var_done", "var_eps_done", "rstd_done", "xn_done", "xb_done"))
        s_tl = sem("transposed_lo_done")
        s_pp, s_pe = sem("projection_in_psum"), sem("projection_kept")
        s_r, s_mid, s_lo = sem("remainder_done"), sem("mid_done"), sem("lo_done")
        s_s, s_red, s_hi, s_mp, s_mt, s_mte, s_st, s_exp, s_pv, s_rc, s_nrm = (sem(n) for n in (
            "scores_ready", "max_done", "max_hi_done", "max_parts_done", "max_transposed", "max_kept",
            "scoresT_ready", "exp_done", "pv_ready", "recip_done", "attn_normed"))
        s_uv, s_tpv = sem("pvT_kept"), sem("pv_transposed")
        s_at, s_ath, s_ate = sem("attn_transposed"), sem("attnT_hi_done"), sem("attnT_kept")
        s_y, s_x2 = sem("wo_ready"), sem("x2_done")

        CONSTS = 3 + E + 1 + 2 + 2 + 3
        SETUP_DVE = C + 7 + 4

        SLICES = [((1, 4), (1, 5)), ((1, 6), (1, 7)), (), ((1, 8),), (), ((1, 9),), ((2, 0), (2, 1)), ((2, 2), (2, 3))]

        weight_banks = []
        for dst in (wqT, wkT, wvT, woT):
            weight_banks.append((dst[0][:].rearrange("p c d -> p (c d)").bitcast(F32R), C * D))
        weight_banks.append((cols[:], 3 * C + MC))
        weight_banks.append((ecols[:].rearrange("p c e -> p (c e)"), C * 3 * E))

        FIRST, LAST = 0, PAIRS - 1

        def pairs(engine, group_step):
            for n in range(2):
                group_step(FIRST, n, True, False)
            with engine.Fori(FIRST + 1, LAST) as pair:
                for n in range(2):
                    group_step(pair, n, False, False)
            for n in range(2):
                group_step(LAST, n, False, True)

        f_ld = [sem(f"ffn_x2_loaded{n}") for n in range(2)]
        f_st = [sem(f"ffn_out_stored{n}") for n in range(2)]
        (f_bn, f_mv, f_v1, f_r1, f_v2, f_v3, f_v4, f_r2, f_r12, f_xn) = (sem("ffn_" + n) for n in (
            "bn_stats", "mean_var", "var_eps", "rstd1", "var2a", "var2", "var2_eps", "rstd2", "rstd12", "xhat"))
        (f_tr, f_tre, f_g, f_gk, f_oh, f_ot, f_ote, f_h, f_he, f_y, f_out) = (sem("ffn_" + n) for n in (
            "xhatT_in_psum", "xhatT_kept", "logits_ready", "routing_step", "onehot_done", "onehotT_in_psum",
            "onehotT_kept", "hidden_in_psum", "hidden_kept", "out_in_psum", "out_done"))
        f_hh, f_hl, f_xh, f_xl, f_cp = (sem("ffn_" + n) for n in (
            "hidden_hi_done", "hidden_lo_done", "xhatT_hi_done", "xhatT_lo_done", "x2_copied"))
        f_gl, f_gle = sem("ffn_logitsT_in_psum"), sem("ffn_logitsT_kept")
        GK = 5
        tr_ps = pp_ps
        h_ps = [s_ps[:, 0:512], s_ps[:, 512:1024]]
        o_ps = [st_ps[:, 0:D], st_ps[:, 512:512 + D]]
        gT_ps = t_ps[:, 0:P]
        g_ps = t_ps[:, P:P + GB * EP].rearrange("p (b e) -> p b e", e=EP)[:, :, 0:E]
        onehotT_ps = pv_ps[0:3 * EP, 0:GT // 2].bitcast(BF16)

        def ffn_load(sp, pair, n):
            src = x2_v[index(sp, pair * 2 + n)]
            wait(sp, f_xn, at(pair, GB, n - 2, GB))
            wait(sp, f_cp, at(pair, 1, n - 2, 1))
            sp.dma_start(xin[n % 2][:], src).then_inc(f_ld[n % 2], 16)

        def ffn_sync(sp):
            def store(pair, n):
                dst = out_v[index(sp, pair * 2 + n)]
                sp.wait_ge(f_out, at(pair, GB, n, GB))
                sp.dma_start(dst, xb[n % 2][:]).then_inc(f_st[n % 2], 16)

            def group(pair, n, is_first, is_last):
                if not is_last:
                    ffn_load(sp, pair, n + 2)
                store(pair, n)

            pairs(sp, group)
            for n in range(2):
                sp.wait_ge(f_st[n], 16 * PAIRS)

        def ffn_pool(pool):
            g = nc.gpsimd

            def norm(pair, n):
                one = at(pair, 1, n, 1)
                pool.wait_ge(f_mv, at(pair, GB, n, GB))
                g.tensor_tensor(ve[:], mv[:, :, 1], eps[:], ALU.add).then_inc(f_v1, 1)
                pool.wait_ge(f_v1, one)
                g.tensor_tensor(rstd[:], ve[:], neg_half[:], ALU.pow).then_inc(f_r1, 1)
                pool.wait_ge(f_r1, one)
                g.tensor_tensor(ve[:], mv[:, :, 1], rstd[:], ALU.mult).then_inc(f_v2, 1)
                pool.wait_ge(f_v2, one)
                g.tensor_tensor(rstd2[:], ve[:], rstd[:], ALU.mult).then_inc(f_v3, 1)
                pool.wait_ge(f_v3, one)
                g.tensor_tensor(ve[:], rstd2[:], eps[:], ALU.add).then_inc(f_v4, 1)
                pool.wait_ge(f_v4, one)
                g.tensor_tensor(rstd2[:], ve[:], neg_half[:], ALU.pow).then_inc(f_r2, 1)
                pool.wait_ge(f_r2, one)
                g.tensor_tensor(rstd[:], rstd[:], rstd2[:], ALU.mult).then_inc(f_r12, 1)

            def lo_of_xT(pair, n):
                pool.wait_ge(f_xh, at(pair, C, n, C))
                g.tensor_tensor(xhT_lo[n % 2][:, 1, :].bitcast(F32R), xhT[n % 2][:, 1, :], xhT_hi[n % 2][:, 1, :],
                                ALU.subtract).then_inc(f_xl, 1)

            norm(0, 0)
            norm(0, 1)
            lo_of_xT(0, 0)

            def group(pair, n, is_first, is_last):
                more = not (is_last and n == 1)
                if not is_last:
                    norm(pair, n + 2)
                if more:
                    lo_of_xT(pair, n + 1)

            pairs(pool, group)

        def ffn_act(act):
            a = nc.scalar

            def keep_xT(pair, n, c):
                act.wait_ge(f_tr, at(pair, C, n, c + 1))
                a.copy(xhT[n % 2][:, c, :], tr_ps[c][:]).then_inc(f_tre, 1)

            def keep_onehot(pair, n):
                act.wait_ge(f_ot, at(pair, 1, n, 1))
                a.activation(offhotT[n % 2][:], onehotT_ps, ACT.Copy, bias=-1.0).then_inc(f_ote, 1)

            def gelu(pair, n, m):
                act.wait_ge(f_h, at(pair, MC, n, m + 1))
                wait(act, f_hl, at(pair, MC, n - 1, m + 1))
                a.activation(hidden32[m], h_ps[m % 2], ACT.Gelu, bias=c1[:, m:m + 1]).then_inc(f_he, 1)

            def copy(pair, n):
                act.wait_ge(f_ld[n % 2], (pair + n // 2 + 1) * 16)
                wait(act, f_st[n % 2], (pair + n // 2) * 16)
                a.copy(xb[n % 2][:], xin[n % 2][:]).then_inc(f_cp, 1)

            for c in range(C):
                keep_xT(0, 0, c)
            act.wait_ge(st_x2[0], 16 * PAIRS)
            copy(0, 0)

            def group(pair, n, is_first, is_last):
                keep_onehot(pair, n)
                for m in range(MC):
                    gelu(pair, n, m)
                    if m == 1:
                        a.copy(onehotT[n % 2][:], onehotT_ps)
                    if m == 1 and not (is_last and n == 1):
                        if is_first and n == 0:
                            act.wait_ge(st_x2[1], 16 * PAIRS)
                        copy(pair, n + 1)
                if not (is_last and n == 1):
                    for c in range(C):
                        keep_xT(pair, n + 1, c)

            pairs(act, group)

        def ffn_stats_of(dve, pair, n):
            v = nc.vector
            dve.wait_ge(f_ld[n % 2], (pair + n // 2 + 1) * 16)
            for b in range(GB):
                v.bn_stats(stats[:, b, :], xin[n % 2][:, b, :]).then_inc(f_bn, 1)
            for b in range(GB):
                count = in_register(dve, at(pair, GB, n, b + 1))
                dve.wait_ge(s_const, 1)
                dve.wait_ge(f_bn, count)
                v.bn_aggr(mv[:, b, :], stats[:, b, :]).then_inc(f_mv, 1)

        def ffn_normalise(dve, pair, n):
            v = nc.vector
            dve.wait_ge(f_r12, at(pair, 1, n, 1))
            wait(dve, f_tr, at(pair, C, n - 1, C))
            for b in range(GB):
                v.tensor_scalar(xn[:, b, :], xin[n % 2][:, b, :], mv[:, b, 0:1], rstd[:, b:b + 1],
                                ALU.subtract, ALU.mult).then_inc(f_xn, 1)

        def ffn_dve(dve):
            v = nc.vector

            def route(pair, n):
                dve.wait_ge(f_g, at(pair, 1, n, 1))
                lg = g_ps
                topb = top[:].unsqueeze(2).broadcast_to([P, GB, E])
                v.tensor_reduce(top[:], lg, AX_X, ALU.max).then_inc(f_gk, 1)
                dve.wait_ge(f_gk, at(pair, GK, n, 1))
                v.tensor_tensor(hit[:], lg, topb, ALU.is_equal).then_inc(f_gk, 1)
                dve.wait_ge(f_gk, at(pair, GK, n, 2))
                v.tensor_tensor(first[:], hit[:], rank[:].unsqueeze(1).broadcast_to([P, GB, E]),
                                ALU.mult).then_inc(f_gk, 1)
                dve.wait_ge(f_gk, at(pair, GK, n, 3))
                v.tensor_reduce(top[:], first[:], AX_X, ALU.max).then_inc(f_gk, 1)
                dve.wait_ge(f_gk, at(pair, GK, n, 4))
                wait(dve, f_ot, at(pair, 1, n, 0))
                v.tensor_tensor(onehot[:, :, :, 0:E], first[:].unsqueeze(2).broadcast_to([P, GB, 3, E]),
                                top[:].unsqueeze(2).unsqueeze(3).broadcast_to([P, GB, 3, E]),
                                ALU.is_equal).then_inc(f_gk, 1)

            def keep_logits(pair, n):
                dve.wait_ge(f_gl, at(pair, 1, n, 1))
                v.tensor_copy(logitT[:], gT_ps).then_inc(f_gle, 1)

            def add(pair, n, b):
                dve.wait_ge(f_y, at(pair, GB, n, b + 1))
                if b == 0:
                    dve.wait_ge(f_cp, at(pair, 1, n, 1))
                xr = xb[n % 2][:, b, :]
                v.tensor_tensor(xr, xr, o_ps[b % 2], ALU.add).then_inc(f_out, 1)

            def split_hidden(pair, n, m):
                dve.wait_ge(f_he, at(pair, MC, n, m + 1))
                hi, lo = hT_hi[n % 2][:, m, :], hT_lo[n % 2][:, m, :]
                v.tensor_copy(hi.bitcast(F32R), hidden32[m]).then_inc(f_hh, 1)
                dve.wait_ge(f_hh, at(pair, MC, n, m + 1))
                v.tensor_tensor(lo.bitcast(F32R), hidden32[m], hi, ALU.subtract).then_inc(f_hl, 1)

            def split_xT(pair, n):
                for c in range(C):
                    dve.wait_ge(f_tre, at(pair, C, n, c + 1))
                    v.tensor_copy(xhT_hi[n % 2][:, c, :].bitcast(F32R), xhT[n % 2][:, c, :]).then_inc(f_xh, 1)
                dve.wait_ge(f_xh, at(pair, C, n, 1))
                v.tensor_tensor(xhT_lo[n % 2][:, 0, :].bitcast(F32R), xhT[n % 2][:, 0, :], xhT_hi[n % 2][:, 0, :],
                                ALU.subtract).then_inc(f_xl, 1)

            split_xT(0, 0)
            keep_logits(0, 0)
            route(0, 0)

            def group(pair, n, is_first, is_last):
                more = not (is_last and n == 1)
                if more:
                    ffn_normalise(dve, pair, n + 1)
                for m in range(MC):
                    split_hidden(pair, n, m)
                if not is_last:
                    ffn_stats_of(dve, pair, n + 2)
                add(pair, n, 0)
                if more:
                    split_xT(pair, n + 1)
                add(pair, n, 1)
                if more:
                    keep_logits(pair, n + 1)
                add(pair, n, 2)
                if more:
                    route(pair, n + 1)
                add(pair, n, 3)

            pairs(dve, group)

        def ffn_pe(pe):
            t = nc.tensor

            def turn(pair, n, c):
                wait(pe, f_tre, at(pair, C, n - 1, c + 1))
                for b in range(GB):
                    if c == 0:
                        pe.wait_ge(f_xn, at(pair, GB, n, b + 1))
                    mm = t.transpose(tr_ps[c][:, b * T:(b + 1) * T], xn[:, b, c * P:(c + 1) * P], ident[:])
                mm.then_inc(f_tr, 1)

            def gate(pair, n):
                pe.wait_ge(f_tre, at(pair, C, n, C))
                wait(pe, f_gk, at(pair, GK, n, 0))
                for c in range(C):
                    for b in range(GB):
                        mm = t.matmul(gT_ps[b * EP:(b + 1) * EP, :], wg_pad[:, c, :], xhT[n % 2][:, c, b * T:(b + 1) * T],
                                      start=(c == 0), stop=(c == C - 1))
                mm.then_inc(f_gl, 1)

            def turn_logits(pair, n):
                pe.wait_ge(f_gle, at(pair, 1, n, 1))
                t.transpose(t_ps[:, P:2 * P], logitT[:], ident[:]).then_inc(f_g, 1)

            def turn_onehot(pair, n):
                pe.wait_ge(f_gk, at(pair, GK, n, GK))
                wait(pe, f_ote, at(pair, 1, n, 0))
                for b in range(GB):
                    mm = t.transpose(onehotT_ps[:, b * T:(b + 1) * T], onehot[:, b, :, :], ident_bf[:])
                mm.then_inc(f_ot, 1)

            def hidden(pair, n, m):
                wait(pe, f_he, at(pair, MC, n, m - 1))
                e = slice(EC * m, EC * (m + 1))
                if m == 0:
                    pe.wait_ge(f_xh, at(pair, C, n, C))
                for k, (w, x) in enumerate(((w1_hi, xhT_hi), (w1_lo, xhT_hi), (w1_hi, xhT_lo))):
                    if m == 0 and k == 2:
                        pe.wait_ge(f_xl, at(pair, C, n, C))
                    for c in range(C):
                        t.matmul(h_ps[m % 2], w[:, c, e, :].bitcast(F32R), x[n % 2][:, c, :].bitcast(F32R),
                                 start=(k == 0 and c == 0), stop=False)

            def mask(pair, n, m):
                if m == 0:
                    pe.wait_ge(f_ote, at(pair, 1, n, 1))
                t.matmul(h_ps[m % 2], far_sel[:, EC * m:EC * (m + 1), :], offhotT[n % 2][0:E, :],
                         start=False, stop=True).then_inc(f_h, 1)

            def output(pair, n, b):
                o = o_ps[b % 2]
                tok = slice(b * T, (b + 1) * T)
                wait(pe, f_out, at(pair, GB, n, b - 1))
                for m in range(MC):
                    if b == 0:
                        pe.wait_ge(f_hl, at(pair, MC, n, m + 1))
                    for k, (h, w) in enumerate(((hT_hi, w2_hi), (hT_hi, w2_lo), (hT_lo, w2_hi))):
                        t.matmul(o, h[n % 2][:, m, tok].bitcast(F32R), w[:, m, :].bitcast(F32R),
                                 start=(m == 0 and k == 0), stop=False)
                t.matmul(o, onehotT[n % 2][:, tok], b2p[:], start=False, stop=True).then_inc(f_y, 1)

            pe.wait_ge(s_x2, GROUPS * GB)
            for c in range(C):
                turn(0, 0, c)
            gate(0, 0)
            turn_logits(0, 0)

            def group(pair, n, is_first, is_last):
                more = not (is_last and n == 1)
                hidden(pair, n, 0)
                turn_onehot(pair, n)
                hidden(pair, n, 1)
                mask(pair, n, 0)
                mask(pair, n, 1)
                for m in range(2, MC):
                    hidden(pair, n, m)
                    mask(pair, n, m)
                if more:
                    for c in range(C):
                        turn(pair, n + 1, c)
                for b in range(GB):
                    output(pair, n, b)
                    if b == 1 and more:
                        gate(pair, n + 1)
                    if b == 2 and more:
                        turn_logits(pair, n + 1)

            pairs(pe, group)

        def clear_pad(engine, z, n):
            engine.memset(packed[z][n][KP:P, :, :].rearrange("p h t -> p (h t)"), 0.0).then_inc(s_pad, 1)

        block = stack.enter_context(nc.Block())

        @block.sync
        def _(sp):
            def load_x(pair, g):
                src = x_v[index(sp, pair * 2 + g)]
                wait(sp, s_xb, at(pair, 1, g - 2, 1))
                sp.dma_start(xin[g % 2][:], src).then_inc(ld_x[g % 2], 16)

            def load_c(pair, g):
                src = c_v[index(sp, pair * 2 + g)]
                wait(sp, s_pp, at(pair, ITEMS, g - 1, 2))
                sp.dma_start(cin[:], src).then_inc(ld_c, 16)

            def store_x2(pair, g):
                dst = x2_v[index(sp, pair * 2 + g)]
                wait(sp, s_x2, at(pair, GB, g, GB))
                sp.dma_start(dst, xb[g % 2][:]).then_inc(st_x2[g % 2], 16)

            def store_parts(pair, g, z):
                wait(sp, s_lo, at(pair, 2, g, z + 1))
                there = parts_dram[z][g % 2]
                sp.dma_start(there.rearrange("n (c p) t -> p n c t", p=P), parts[z][:]).then_inc(st_parts[z], 16)

            def pack(pair, g, z):
                there = parts_dram[z][g % 2]
                wait(sp, st_parts[z], at(pair, 16, g, 16))
                for n, part in enumerate((Q_PARTS, K_PARTS)[z]):
                    sp.dma_start(packed[z][g % 2][n * DH:(n + 1) * DH, :, :],
                                 there[part].rearrange("(h d) t -> d h t", d=DH)).then_inc(pk[z][g % 2], 16)

            for v, t in ((wq, xn[:, 0:C, :]), (wk, xn[:, C:2 * C, :]),
                         (wv, z32[0][:, 0, :].rearrange("p (c d) -> p c d", c=C)),
                         (wo, z32[0][:, 1, :].rearrange("p (c d) -> p c d", c=C))):
                sp.dma_start(t, v.rearrange("(c p) d -> p c d", p=P)).then_inc(s_w, 16)
            load_x(0, 0)
            load_c(0, 0)
            for n, v in enumerate((bq, bk, bv)):
                sp.dma_start(rows[n * C:(n + 1) * C, :], v.rearrange("(c p) -> c p", p=P)).then_inc(s_small, 16)
            sp.dma_start(rows[3 * C:3 * C + MC, :], b1.rearrange("(m e) h -> m (e h)", e=EC)).then_inc(s_small, 16)
            for n, v in enumerate((wg, ln_s, ln_b)):
                sp.dma_start(erows[n * E:(n + 1) * E, :], v).then_inc(s_small, 16)
            sp.dma_start(bo_row[:], bo.rearrange("(a d) -> a d", a=1)).then_inc(s_small, 16)
            sp.wait_ge(s_b2z, 1)
            for k in range(3):
                sp.dma_start(b2f[k * EP:k * EP + E, :], b2).then_inc(s_small, 16)
            for c in range(C):
                sp.dma_start(w1s[:, c, :, :], w1[:, c * P:(c + 1) * P, :].rearrange("e p h -> p e h")).then_inc(s_wf, 16)
            sp.dma_start(w2s, w2.rearrange("e h d -> (e h) d").rearrange("(m p) d -> p m d", p=P)).then_inc(s_wf, 16)

            load_x(0, 1)
            load_c(0, 1)
            for z in range(2):
                store_parts(0, 0, z)
            for z in range(2):
                pack(0, 0, z)

            def group(pair, g, is_first, is_last):
                more = not (is_last and g == 1)
                if not is_last:
                    load_x(pair, g + 2)
                    load_c(pair, g + 2)
                if more:
                    for z in range(2):
                        store_parts(pair, g + 1, z)
                        pack(pair, g + 1, z)
                if not (is_first and g == 0):
                    store_x2(pair, g - 1)

            pairs(sp, group)
            for n in range(2):
                sp.wait_ge(s_xb, GROUPS - 1 + n)
                sp.wait_ge(st_x2[n], 16)
                ffn_load(sp, 0, n)
            store_x2(LAST, 1)
            for n in range(2):
                sp.wait_ge(st_x2[n], 16 * PAIRS)
            ffn_sync(sp)

        @block.gpsimd
        def _(pool):
            g = nc.gpsimd
            g.memset(ident[:], 0.0).then_inc(s_pc, 1)
            g.memset(head_sel[:], 0.0).then_inc(s_pc, 1)
            g.memset(far_sel[:], 0.0).then_inc(s_pc, 1)
            g.memset(neg_half[:], -0.5).then_inc(s_const, 1)
            g.memset(eps[:], EPS).then_inc(s_const, 1)
            g.memset(ones_row[:], 1.0).then_inc(s_const, 1)
            for e in range(E):
                g.memset(rank[:, e:e + 1], float(E - e)).then_inc(s_const, 1)
            pool.wait_ge(s_pc, 3)
            g.affine_select(out=ident[:], in_=ident[:], compare_op=ALU.not_equal, fill=1.0, base=0,
                            pattern=[[-1, P]], channel_multiplier=1).then_inc(s_pc, 1)
            g.affine_select(out=head_sel[:], in_=head_sel[:], compare_op=ALU.not_equal, fill=1.0, base=0,
                            pattern=[[-1, HC], [0, P]], channel_multiplier=1).then_inc(s_pc, 1)
            g.affine_select(out=far_sel[:], in_=far_sel[:], compare_op=ALU.not_equal, fill=-FAR, base=0,
                            pattern=[[-1, MC * EC], [0, HID]], channel_multiplier=1).then_inc(s_const, 1)
            for n in range(2):
                g.memset(v1[n][:], 1.0).then_inc(s_const, 1)
            pool.wait_ge(s_pc, 5)
            g.affine_select(out=head_sel[:], in_=head_sel[:], compare_op=ALU.not_equal, fill=1.0, base=-HC,
                            pattern=[[-1, HC], [0, P]], channel_multiplier=1).then_inc(s_const, 1)
            g.tensor_copy(ident_bf[:], ident[:]).then_inc(s_const, 1)

            def norm(pair, n):
                pool.wait_ge(s_mv, at(pair, GB, n, GB))
                g.tensor_tensor(ve[:], mv[:, :, 1], eps[:], ALU.add).then_inc(s_ve, 1)
                pool.wait_ge(s_ve, at(pair, 1, n, 1))
                g.tensor_tensor(rstd[:], ve[:], neg_half[:], ALU.pow).then_inc(s_rstd, 1)

            def lo(pair, n, z):
                pool.wait_ge(s_mid, at(pair, 2, n, z + 1))
                g.tensor_tensor(parts[z][:, 2, :, :], z32[z][:], parts[z][:, 1, :, :], ALU.subtract).then_inc(s_lo, 1)

            def residual(pair, n):
                pool.wait_ge(s_xn, at(pair, GB, n, GB))
                wait(pool, st_x2[n % 2], (pair + n // 2) * 16)
                for b in range(GB):
                    last = g.tensor_tensor(xb[n % 2][:, b, :], xin[n % 2][:, b, :], bo_all[:], ALU.add)
                last.then_inc(s_xb, 1)

            norm(0, 0)
            pool.wait_ge(s_bo, 1)
            residual(0, 0)
            for z in range(2):
                lo(0, 0, z)
            norm(0, 1)

            def group(pair, n, is_first, is_last):
                if not (is_last and n == 1):
                    for z in range(2):
                        lo(pair, n + 1, z)
                if not is_last:
                    norm(pair, n + 2)
                if not (is_last and n == 1):
                    residual(pair, n + 1)

            pairs(pool, group)
            ffn_pool(pool)

        @block.scalar
        def _(act):
            a = nc.scalar

            def keep_max(pair, n, u):
                act.wait_ge(s_mt, at(pair, UNITS, n, u + 1))
                a.copy(negmaxT[u % 2][0:2 * HC, :], maxT_ps).then_inc(s_mte, 1)

            def keep_pvT(pair, n, b):
                act.wait_ge(s_pv, at(pair, UNITS, n, C * (b + 1)))
                wait(act, s_tpv, at(pair, GB, n, b))
                a.copy(uvT[:], pv_ps[:]).then_inc(s_uv, 1)

            def item(pair, n, k):
                act.wait_ge(s_pp, at(pair, ITEMS, n, k + 1))
                ps = pp_ps[k % 2]
                if k < 4:
                    last = a.copy((cT, xT)[k // 2][0][:, k % 2, :].bitcast(F32R), ps[:])
                elif k < 8:
                    z, m = (k - 4) // 2, k % 2
                    if m == 0:
                        wait(act, s_lo, at(pair, 2, n - 1, z + 1))
                        wait(act, st_parts[z], at(pair, 16, n - 1, 16))
                    bias = cols[:, z * C + m:z * C + m + 1]
                    a.activation(z32[z][:, m, :], ps[:], ACT.Identity, bias=bias)
                    last = a.activation(parts[z][:, 0, m, :], ps[:], ACT.Identity, bias=bias)
                else:
                    b = 2 * (k - 8)
                    last = a.copy(v1[n % 2][:, b:b + 2, :, 0:DH],
                                  ps[:].rearrange("p (b h d) -> p b h d", b=2, d=DH))
                last.then_inc(s_pe, 1)

            def mid(pair, n, z):
                act.wait_ge(s_r, at(pair, 2, n, z + 1))
                a.copy(parts[z][:, 1, :, :], z32[z][:]).then_inc(s_mid, 1)

            def exp(pair, n, u):
                act.wait_ge(s_st, at(pair, UNITS, n, u + 1))
                wait(act, s_pv, at(pair, UNITS, n, u - 1))
                a.activation(pT[u % 2][:], st_ps[:], ACT.Exp, scale=DH ** -0.5).then_inc(s_exp, 1)

            def items(pair, n, u, is_last):
                for ahead, k in SLICES[u]:
                    if not is_last or n + ahead < 2:
                        item(pair, n + ahead, k)

            for k, (dst, width) in enumerate(weight_banks):
                act.wait_ge(s_wt, k + 1)
                a.copy(dst, pp_ps[k % 2][0:P, 0:width]).then_inc(s_wtc, 1)
            act.wait_ge(s_bo, 1)

            for k in range(ITEMS):
                item(0, 0, k)
                if k == 8:
                    mid(0, 0, 0)
            mid(0, 0, 1)
            for k in range(4):
                item(0, 1, k)
            act.wait_ge(s_set, SETUP_DVE)

            def group(pair, n, is_first, is_last):
                more = not (is_last and n == 1)
                for u in range(UNITS):
                    keep_max(pair, n, u)
                    if more and u == 2:
                        mid(pair, n + 1, 1)
                    if u % 2 == 1:
                        if u > 1:
                            keep_pvT(pair, n, u // 2 - 1)
                        elif not (is_first and n == 0):
                            keep_pvT(pair, n - 1, GB - 1)
                    if u > 1:
                        exp(pair, n, u)
                    items(pair, n, u, is_last)
                    if u <= 1:
                        exp(pair, n, u)
                    if more and u == 0:
                        mid(pair, n + 1, 0)

            pairs(act, group)
            keep_pvT(LAST, 1, GB - 1)
            ffn_act(act)

        @block.vector
        def _(dve):
            v = nc.vector
            step = [0]

            def setup(ins):
                step[0] += 1
                ins.then_inc(s_set, 1)
                dve.wait_ge(s_set, step[0])

            def stats_of(pair, n):
                dve.wait_ge(ld_x[n % 2], (pair + n // 2 + 1) * 16)
                for b in range(GB):
                    v.bn_stats(stats[:, b, :], xin[n % 2][:, b, :]).then_inc(s_bn, 1)
                for b in range(GB):
                    count = in_register(dve, at(pair, GB, n, b + 1))
                    dve.wait_ge(s_const, 1)
                    dve.wait_ge(s_bn, count)
                    v.bn_aggr(mv[:, b, :], stats[:, b, :]).then_inc(s_mv, 1)

            def normalise(pair, n):
                dve.wait_ge(s_rstd, at(pair, 1, n, 1))
                wait(dve, s_pp, at(pair, ITEMS, n - 1, 4))
                for b in range(GB):
                    v.tensor_scalar(xn[:, b, :], xin[n % 2][:, b, :], mv[:, b, 0:1], rstd[:, b:b + 1],
                                    ALU.subtract, ALU.mult).then_inc(s_xn, 1)

            def remainder(pair, n, z):
                dve.wait_ge(s_pe, at(pair, ITEMS, n, 6 + 2 * z))
                v.tensor_tensor(z32[z][:], z32[z][:], parts[z][:, 0, :, :], ALU.subtract).then_inc(s_r, 1)

            def maxima(pair, n, u):
                dve.wait_ge(s_s, at(pair, UNITS, n, u + 1))
                v.tensor_reduce(negmax[u % 2][:], s_ps[:].rearrange("p (h s) -> p h s", s=P), AX_X, ALU.max,
                                negate=True).then_inc(s_red, 1)
                dve.wait_ge(s_red, at(pair, UNITS, n, u + 1))
                wait(dve, s_mt, at(pair, UNITS, n, u - 1))
                v.tensor_copy(negmax_p[u % 2][:, 0:HC], negmax[u % 2][:]).then_inc(s_hi, 1)
                dve.wait_ge(s_hi, at(pair, UNITS, n, u + 1))
                v.tensor_tensor(negmax_p[u % 2][:, HC:2 * HC], negmax[u % 2][:], negmax_p[u % 2][:, 0:HC],
                                ALU.subtract).then_inc(s_mp, 1)

            def norm(pair, n, b):
                dve.wait_ge(s_tpv, at(pair, GB, n, b + 1))
                v.reciprocal(recip[:], pv[:, :, DH]).then_inc(s_rc, 1)
                dve.wait_ge(s_rc, at(pair, GB, n, b + 1))
                wait(dve, s_at, at(pair, GB, n, b))
                v.tensor_tensor(attn[:], pv[:, :, 0:DH], recip[:].unsqueeze(2).broadcast_to([P, H, DH]),
                                ALU.mult).then_inc(s_nrm, 1)

            def keep_attn(pair, n, b):
                dve.wait_ge(s_at, at(pair, GB, n, b + 1))
                wait(dve, s_y, at(pair, GB, n, b - 1))
                hi, lo = aT[b % 2]
                from_ps = attnT_ps.rearrange("p (c t) -> p c t", c=C)
                v.tensor_copy(hi[:].bitcast(F32R), from_ps).then_inc(s_ath, 1)
                dve.wait_ge(s_ath, at(pair, GB, n, b + 1))
                v.tensor_tensor(lo[:].bitcast(F32R), from_ps, hi[:], ALU.subtract).then_inc(s_ate, 1)

            def lower(pair, n, k):
                hi, lo = (cT, xT)[k // 2]
                dve.wait_ge(s_pe, at(pair, ITEMS, n, k + 1))
                v.tensor_tensor(lo[:, k % 2, :].bitcast(F32R), pp_ps[k % 2][:], hi[:, k % 2, :],
                                ALU.subtract).then_inc(s_tl, 1)

            def residual(pair, n, b):
                dve.wait_ge(s_y, at(pair, GB, n, b + 1))
                if b == 0:
                    dve.wait_ge(s_xb, at(pair, 1, n, 1))
                xr = xb[n % 2][:, b, :]
                v.tensor_tensor(xr, xr, y_ps(b), ALU.add).then_inc(s_x2, 1)

            v.memset(b2f[:], 0.0).then_inc(s_b2z, 1)
            v.memset(onehot[:].rearrange("p b k e -> p (b k e)"), 0.0).then_inc(s_const, 1)
            clear_pad(v, 0, 0)
            for n in range(2):
                v.memset(negmaxT[n][:].bitcast(F32), 0.0).then_inc(s_const, 1)
            for k, w in enumerate((wqT, wkT, wvT, woT)):
                dve.wait_ge(s_wtc, k + 1)
                v.tensor_tensor(w[1][:].rearrange("p c d -> p (c d)").bitcast(F32R), pp_ps[k % 2][:],
                                w[0][:].rearrange("p c d -> p (c d)"), ALU.subtract).then_inc(s_wl, 1)
            stats_of(0, 0)
            dve.wait_ge(s_wt, len(weight_banks) + 1)
            dve.wait_ge(s_wtc, len(weight_banks))
            for m in range(MC):
                for e in range(EC):
                    r = slice(e * HID, (e + 1) * HID)
                    v.tensor_tensor(c1[r, m:m + 1], pp_ps[0][r, EC * m + e:EC * m + e + 1],
                                    cols[r, 3 * C + m:3 * C + m + 1], ALU.add)
            dve.wait_ge(s_wt, len(weight_banks) + 2)
            v.tensor_copy(bo_all[:], pp_ps[1][:, 0:D]).then_inc(s_bo, 1)

            normalise(0, 0)
            for k in range(4):
                lower(0, 0, k)
            for c in range(C):
                ls = ecols[:, c, E:2 * E].unsqueeze(2).broadcast_to([P, E, HID])
                setup(v.tensor_tensor(w1s[:, c, :, :], w1s[:, c, :, :], ls, ALU.mult))
            for full, upper, rest in ((w1s.rearrange("p c e h -> p (c e h)"), w1_hi[:].rearrange("p c e h -> p (c e h)"),
                                  w1_lo[:].rearrange("p c e h -> p (c e h)")),
                                 (w2s.rearrange("p m d -> p (m d)"), w2_hi[:].rearrange("p m d -> p (m d)"),
                                  w2_lo[:].rearrange("p m d -> p (m d)"))):
                setup(v.tensor_copy(upper.bitcast(F32R), full))
                setup(v.tensor_tensor(rest.bitcast(F32R), full, upper, ALU.subtract))
            setup(v.memset(wg_pad[:].rearrange("p c e -> p (c e)"), 0.0))
            setup(v.tensor_copy(wg_pad[:, :, 0:E], ecols[:, :, 0:E]))
            setup(v.tensor_copy(b2p[:], b2f[:]))
            setup(v.tensor_tensor(b2r[:], b2f[:], b2p[:], ALU.subtract))
            for k in (1, 2):
                setup(v.tensor_copy(b2p[k * EP:(k + 1) * EP, :], b2r[k * EP:(k + 1) * EP, :]))
            r = slice(2 * EP, 3 * EP)
            setup(v.tensor_tensor(b2p[r, :], b2r[r, :], b2p[r, :], ALU.subtract))
            remainder(0, 0, 0)
            remainder(0, 0, 1)
            clear_pad(v, 1, 0)
            stats_of(0, 1)
            normalise(0, 1)
            for k in range(4):
                lower(0, 1, k)
            clear_pad(v, 0, 1)
            clear_pad(v, 1, 1)
            maxima(0, 0, 0)

            def group(pair, n, is_first, is_last):
                more = not (is_last and n == 1)
                for u in range(UNITS):
                    if u == 0 and not (is_first and n == 0):
                        residual(pair, n - 1, GB - 2)
                    if u + 1 < UNITS:
                        maxima(pair, n, u + 1)
                    elif more:
                        maxima(pair, n + 1, 0)
                    if u == 2 and not (is_first and n == 0):
                        residual(pair, n - 1, GB - 1)
                    if u > 2 and u % 2 == 0:
                        residual(pair, n, u // 2 - 2)
                    if more and u == 0:
                        remainder(pair, n + 1, 0)
                    if not is_last and u == 0:
                        stats_of(pair, n + 2)
                    if not is_last and u == 6:
                        for k in range(2):
                            lower(pair, n + 2, k)
                    if u % 2 == 1:
                        done = (n, u // 2 - 1) if u > 1 else (n - 1, GB - 1)
                        there = u > 1 or not (is_first and n == 0)
                        if there:
                            norm(pair, *done)
                        if not is_last and u == 7:
                            lower(pair, n + 2, 2)
                        if there:
                            keep_attn(pair, *done)
                        if not is_last and u == 7:
                            lower(pair, n + 2, 3)
                        if more and u == 1:
                            remainder(pair, n + 1, 1)
                    if not is_last and u == 4:
                        normalise(pair, n + 2)
                    if not more and u == 5:
                        ffn_stats_of(dve, 0, 0)
                    if not more and u == 6:
                        dve.wait_ge(s_pp, ITEMS * (GROUPS - 1) + 4)
                        ffn_normalise(dve, 0, 0)
                    if not more and u == 7:
                        ffn_stats_of(dve, 0, 1)

            pairs(dve, group)
            residual(LAST, 1, GB - 2)
            norm(LAST, 1, GB - 1)
            keep_attn(LAST, 1, GB - 1)
            residual(LAST, 1, GB - 1)
            ffn_dve(dve)

        @block.tensor
        def _(pe):
            t = nc.tensor

            def scores(pair, n, u):
                b, m = u // C, u % C
                tok = slice(b * T, (b + 1) * T)
                if u == 0:
                    for z in range(2):
                        pe.wait_ge(pk[z][n % 2], (pair + n // 2 + 1) * PACK)
                wait(pe, s_red, at(pair, UNITS, n, u))
                for j in range(HC):
                    h = m * HC + j
                    mm = t.matmul(s_ps[:, j * P:(j + 1) * P], packed[0][n % 2][:, h, tok],
                                  packed[1][n % 2][:, h, tok], start=True, stop=True)
                mm.then_inc(s_s, 1)

            def turn_max(pair, n, u):
                pe.wait_ge(s_mp, at(pair, UNITS, n, u + 1))
                if u % 2 == 0:
                    wait(pe, s_ate, at(pair, GB, n, u // 2 - 1))
                t.transpose(maxT_ps, negmax_p[u % 2][:], ident_bf[:]).then_inc(s_mt, 1)

            def turn_attn(pair, n, b):
                pe.wait_ge(s_nrm, at(pair, GB, n, b + 1))
                for c in range(C):
                    mm = t.transpose(attnT_ps[:, c * P:(c + 1) * P], attn[:, c * HC:(c + 1) * HC, :], ident[:])
                mm.then_inc(s_at, 1)

            def scoresT(pair, n, u):
                b, m = u // C, u % C
                tok = slice(b * T, (b + 1) * T)
                pe.wait_ge(s_mte, at(pair, UNITS, n, u + 1))
                wait(pe, s_exp, at(pair, UNITS, n, u))
                for j in range(HC):
                    h = m * HC + j
                    o = st_ps[:, j * P:(j + 1) * P]
                    t.matmul(o, packed[1][n % 2][:, h, tok], packed[0][n % 2][:, h, tok],
                             start=True, stop=False)
                    mm = t.matmul(o, head_sel[:, j, :], negmaxT[u % 2][:], start=False, stop=True)
                mm.then_inc(s_st, 1)

            def values(pair, n, u):
                b, m = u // C, u % C
                pe.wait_ge(s_exp, at(pair, UNITS, n, u + 1))
                if m == 0:
                    wait(pe, s_nrm, at(pair, GB, n, b))
                if u == 0:
                    pe.wait_ge(s_pe, at(pair, ITEMS, n, ITEMS))
                for j in range(HC):
                    h = m * HC + j
                    strip, block = h % 4 * HP, h // 4 * P
                    mm = t.matmul(pv_ps[strip:strip + HP, block:block + P], v1[n % 2][:, b, h, :],
                                  pT[u % 2][:, j * P:(j + 1) * P], start=True, stop=True)
                mm.then_inc(s_pv, 1)

            def turn_pv(pair, n, b):
                pe.wait_ge(s_uv, at(pair, GB, n, b + 1))
                for k in range(4):
                    mm = t.transpose(pv_ps[:, k * P:(k + 1) * P], uvT[:, k * P:(k + 1) * P], ident[:])
                mm.then_inc(s_tpv, 1)

            def project_out(pair, n, b, now, keeps):
                pe.wait_ge(s_ath, at(pair, GB, n, b + 1))
                if keeps:
                    pe.wait_ge(s_pe, at(pair, ITEMS, now + 1, keeps))
                if keeps == 4:
                    pe.wait_ge(s_tl, at(pair, 4, now + 1, 4))
                if not keeps:
                    wait(pe, s_x2, at(pair, GB, n, b - 1))
                for i, j in SPLIT:
                    if i == 1:
                        pe.wait_ge(s_ate, at(pair, GB, n, b + 1))
                    for c in range(C):
                        mm = t.matmul(y_ps(b), aT[b % 2][i][:, c, :].bitcast(F32R), woT[j][:, c, :].bitcast(F32R),
                                      start=(c == 0 and i == j), stop=(c == C - 1 and i == 1))
                mm.then_inc(s_y, 1)

            def item(pair, n, k):
                ps = pp_ps[k % 2]
                if k == 0:
                    pe.wait_ge(ld_c, at(pair, 16, n, 16))
                if k == 2:
                    pe.wait_ge(s_xn, at(pair, GB, n, GB))
                wait(pe, s_pe, at(pair, ITEMS, n, k - 1))
                if k in (2, 3):
                    pe.wait_ge(s_tl, at(pair, 4, n, k - 1))
                if k == 4:
                    pe.wait_ge(s_tl, at(pair, 4, n, 4))
                if k == 0:
                    wait(pe, s_x2, at(pair, GB, n - 2, 2))
                if k == 5:
                    wait(pe, s_x2, at(pair, GB, n - 2, 3))
                if k == 8:
                    wait(pe, s_x2, at(pair, GB, n - 2, 4))
                if k == 9:
                    wait(pe, s_x2, at(pair, GB, n - 1, 1))
                if k < 4:
                    for b in range(GB):
                        mm = t.transpose(ps[:, b * T:(b + 1) * T],
                                         (cin, xn)[k // 2][:, b, k % 2 * P:(k % 2 + 1) * P], ident[:])
                elif k < 8:
                    w, src = ((wqT, xT), (wkT, cT))[(k - 4) // 2]
                    for c in range(C):
                        for i, j in SPLIT:
                            mm = t.matmul(ps[:], w[i][:, c, k % 2 * P:(k % 2 + 1) * P].bitcast(F32R),
                                          src[j][:, c, :].bitcast(F32R),
                                          start=(c == 0 and i == j), stop=(c == C - 1 and i == 1))
                else:
                    for b in range(2):
                        tok = (2 * (k - 8) + b) * T
                        for c in range(C):
                            for i, j in SPLIT:
                                mm = t.matmul(ps[:, b * D:(b + 1) * D], cT[i][:, c, tok:tok + T].bitcast(F32R),
                                              wvT[j][:, c, :].bitcast(F32R),
                                              start=(c == 0 and i == j), stop=(c == C - 1 and i == 1))
                mm.then_inc(s_pp, 1)

            def items(pair, n, u, is_last):
                for ahead, k in SLICES[u]:
                    if not is_last or n + ahead < 2:
                        item(pair, n + ahead, k)

            pe.wait_ge(s_pc, 4)
            pe.wait_ge(s_w, 16 * 4)
            sources = [xn[:, 0:C, :], xn[:, C:2 * C, :], z32[0][:, 0, :].rearrange("p (c d) -> p c d", c=C),
                       z32[0][:, 1, :].rearrange("p (c d) -> p c d", c=C)]
            for k, w in enumerate(sources):
                if k >= 2:
                    pe.wait_ge(s_wtc, k - 1)
                    pe.wait_ge(s_wl, k - 1)
                for ci in range(C):
                    for co in range(C):
                        mm = t.transpose(pp_ps[k % 2][:, ci * D + co * P:ci * D + (co + 1) * P],
                                         w[:, co, ci * P:(ci + 1) * P], ident[:])
                mm.then_inc(s_wt, 1)
            pe.wait_ge(s_wtc, 3)
            pe.wait_ge(s_wl, 3)
            pe.wait_ge(s_small, 16 * 11)
            NR = 3 * C + MC
            t.transpose(pp_ps[0][:, 0:NR], rows[:], ident[0:NR, 0:NR]).then_inc(s_wt, 1)
            pe.wait_ge(s_wtc, 4)
            pe.wait_ge(s_wl, 4)
            for c in range(C):
                mm = t.transpose(pp_ps[1][:, c * 3 * E:(c + 1) * 3 * E], erows[:, c * P:(c + 1) * P],
                                 ident[0:3 * E, 0:3 * E])
            mm.then_inc(s_wt, 1)
            pe.wait_ge(s_wtc, 6)
            pe.wait_ge(s_const, CONSTS)
            pe.wait_ge(s_wf, 16 * 3)
            for m in range(MC):
                for c in range(C):
                    mm = t.matmul(pp_ps[0][:, EC * m:EC * (m + 1)], w1s[:, c, EC * m:EC * (m + 1), :],
                                  ecols[:, c, 2 * E + EC * m:2 * E + EC * (m + 1)], start=(c == 0), stop=(c == C - 1))
            mm.then_inc(s_wt, 1)
            for c in range(C):
                for part in range(2):
                    t.matmul(pp_ps[1][:, 0:D], cols[:, 2 * C + c:2 * C + c + 1].broadcast_to([P, P]), woT[part][:, c, :],
                             start=(c == 0 and part == 0), stop=False)
            t.matmul(pp_ps[1][:, 0:D], ones_row[:], bo_row[:], start=False, stop=True).then_inc(s_wt, 1)
            pe.wait_ge(s_bo, 1)

            for k in range(ITEMS):
                item(0, 0, k)
            for k in range(4):
                item(0, 1, k)
            pe.wait_ge(s_set, SETUP_DVE)
            pe.wait_ge(s_pad, 4)
            scores(0, 0, 0)

            def group(pair, n, is_first, is_last):
                more = not (is_last and n == 1)
                for u in range(UNITS):
                    before = not (is_first and n == 0)
                    nxt = (n, u + 1) if u + 1 < UNITS else (n + 1, 0) if more else None
                    done = (n, u // 2 - 1) if u > 1 else (n - 1, GB - 1)
                    turns = u % 2 == 1 and (u > 1 or before)
                    if u % 2 == 1:
                        turn_max(pair, n, u)
                    if nxt:
                        scores(pair, *nxt)
                    if u % 2 == 0:
                        turn_max(pair, n, u)
                    if u % 2 == 0 and (u > 2 or before):
                        turned = (n, u // 2 - 2) if u > 2 else (n - 1, GB - 2 + u // 2)
                        project_out(pair, *turned, n, {0: 4, 2: 7, 4: 8, 6: 9}[u] if more else 0)
                    if u <= 1:
                        items(pair, n, u, is_last)
                        if turns:
                            turn_pv(pair, *done)
                        scoresT(pair, n, u)
                    else:
                        scoresT(pair, n, u)
                        if turns:
                            turn_pv(pair, *done)
                        if u < 6:
                            items(pair, n, u, is_last)
                    if u == 7:
                        items(pair, n, u, is_last)
                    if turns:
                        turn_attn(pair, *done)
                    if u > 0:
                        values(pair, n, u - 1)
                    elif before:
                        values(pair, n - 1, UNITS - 1)
                    if u == 6:
                        items(pair, n, u, is_last)

            pairs(pe, group)
            project_out(LAST, 1, GB - 2, 2, 0)
            values(LAST, 1, UNITS - 1)
            turn_pv(LAST, 1, GB - 1)
            turn_attn(LAST, 1, GB - 1)
            project_out(LAST, 1, GB - 1, 2, 0)
            ffn_pe(pe)


_INS = ['x', 'ctx_1024'] + ['L0_xattn_' + n for n in ('wq_w', 'wq_b', 'wk_w', 'wk_b', 'wv_w', 'wv_b', 'wo_w', 'wo_b')] + \
    ['L0_ffn_' + n for n in ('Wg', 'ln_scale', 'ln_bias', 'W1', 'b1', 'W2', 'b2')]


def kernel(**inputs):
    import numpy as _np
    import concourse.bacc as _bacc
    from concourse import mybir as _mybir
    from concourse.bass_utils import run_bass_kernel_spmd as _run

    nc = _bacc.Bacc("TRN2", target_bir_lowering=False, num_devices=1)
    arrays, args = {}, []
    for name in _INS:
        a = _np.ascontiguousarray(inputs[name])
        arrays[f"in_{name}_dram"] = a
        args.append(nc.dram_tensor(f"in_{name}_dram", a.shape, _mybir.dt.from_np(a.dtype), kind="ExternalInput").ap())
    shape = inputs["x"].shape
    args.append(nc.dram_tensor("out_0_dram", shape, _mybir.dt.float32, kind="ExternalOutput").ap())
    xattn_moe(nc, *args)
    r = _run(nc, [arrays], core_ids=[0])
    return r.results[0]["out_0_dram"]
```
